# Optimizing a Trainium2 kernel written in Bass

```python
import numpy as np
import jax
import jax.numpy as jnp

def _softmax(x, axis=-1):
    return jax.nn.softmax(x, axis=axis)

def _gelu(x):
    return jax.nn.gelu(x, approximate=True)

def _silu(x):
    return jax.nn.silu(x)

def _sigmoid(x):
    return jax.nn.sigmoid(x)

def _layernorm(x, axis=-1, eps=1e-05):
    m = jnp.mean(x, axis=axis, keepdims=True)
    v = jnp.var(x, axis=axis, keepdims=True)
    return (x - m) / jnp.sqrt(v + eps)

def _scatter_add(tgt, idx, src, axis=0):
    return tgt.at[idx].add(src)

def _segment_sum(src, seg, n):
    return jax.ops.segment_sum(src, seg, n)
kernel_name = 'mk_gnn_ffn_d1_gnn_r8_458abf'

def setup_inputs(seed: int=0):
    np.random.seed(seed)
    _w = jnp.asarray

    def _rec_inputs():
        import jax
        import jax.numpy as jnp
        _gk = jax.random.key(seed)
        x = -7.329e-05 + 0.9999 * jax.random.normal(jax.random.fold_in(_gk, 1), (1250, 512), jnp.float32)
        _s = jax.random.randint(jax.random.fold_in(_gk, 2), (20000,), 0, 1250, jnp.int32)
        _d = jax.random.randint(jax.random.fold_in(_gk, 3), (20000,), 0, 1250, jnp.int32)
        _loop = jnp.arange(1250, dtype=jnp.int32)
        src = jnp.concatenate([_s, _d, _loop])
        dst = jnp.concatenate([_d, _s, _loop])
        _o = jnp.argsort(dst, stable=True)
        src = src[_o]
        dst = dst[_o]
        edge_weight = jax.random.uniform(jax.random.fold_in(_gk, 12), (41250,), jnp.float32, 0.0, 0.999998)
        return (x, src, dst, edge_weight)
    x, src, dst, edge_weight = _rec_inputs()

    def _L0_gnn_setup():
        import jax, jax.numpy as jnp
        import numpy as np
        N = 12500
        E = 100000
        IN_FEATS = 512
        N_HIDDEN = 128
        key = jax.random.key(seed)
        k1, k2, k3, k4, k5, k6 = jax.random.split(key, 6)
        inputs = jax.random.normal(k1, (N, IN_FEATS), dtype=jnp.float32)
        edge_index = jax.random.randint(k2, (2, E), 0, N, dtype=jnp.int64)
        edge_attr = jax.random.uniform(k3, (E,), dtype=jnp.float32)
        s_gcn = jnp.sqrt(6.0 / (IN_FEATS + N_HIDDEN)).astype(jnp.float32)
        W_gcn = jax.random.uniform(k4, (IN_FEATS, N_HIDDEN), dtype=jnp.float32, minval=-s_gcn, maxval=s_gcn)
        b_gcn = jnp.zeros((N_HIDDEN,), dtype=jnp.float32)
        s_fc = jnp.sqrt(6.0 / (N_HIDDEN + IN_FEATS)).astype(jnp.float32)
        W_fc = jax.random.uniform(k5, (IN_FEATS, N_HIDDEN), dtype=jnp.float32, minval=-s_fc, maxval=s_fc)
        b_fc = jax.random.uniform(k6, (IN_FEATS,), dtype=jnp.float32, minval=-1.0 / np.sqrt(N_HIDDEN), maxval=1.0 / np.sqrt(N_HIDDEN))
        return {'inputs': inputs, 'edge_index': edge_index, 'edge_attr': edge_attr, 'W_gcn': W_gcn, 'b_gcn': b_gcn, 'W_fc': W_fc, 'b_fc': b_fc}
    _L0_gnn_all = _L0_gnn_setup()
    _L0_gnn_in = {k: v for k, v in _L0_gnn_all.items() if k in ('W_gcn', 'b_gcn', 'W_fc', 'b_fc')}
    del _L0_gnn_all

    def _L0_ffn_setup():
        import jax, jax.numpy as jnp
        import numpy as np
        B, T, D, F, E, TOP_K = (8, 512, 512, 256, 8, 2)

        def _moe_forward(x, Wr, W1, W2):
            b, t, d = x.shape
            e = Wr.shape[1]
            xf = x.reshape(-1, d)
            n = xf.shape[0]
            logits = xf @ Wr
            probs = jax.nn.softmax(logits, axis=-1)
            w, idx = jax.lax.top_k(probs, TOP_K)
            w = w.astype(xf.dtype)
            gates = jnp.zeros((n, e), xf.dtype).at[jnp.arange(n)[:, None], idx].add(w)

            def body(acc, expert):
                w1, w2, g = expert
                h = jax.nn.gelu(xf @ w1, approximate=False)
                return (acc + g[:, None] * (h @ w2), None)
            out, _ = jax.lax.scan(body, jnp.zeros_like(xf), (W1, W2, gates.T))
            return out.reshape(b, t, d)
        key = jax.random.key(seed)
        k1, k2, k3, k4 = jax.random.split(key, 4)
        x = jax.random.normal(k1, (B, T, D), jnp.float32)
        Wr = jax.random.normal(k2, (D, E), jnp.float32) * (1.0 / np.sqrt(D))
        W1 = jax.random.normal(k3, (E, D, F), jnp.float32) * (1.0 / np.sqrt(D))
        W2 = jax.random.normal(k4, (E, F, D), jnp.float32) * (1.0 / np.sqrt(F))
        return {'x': x, 'Wr': Wr, 'W1': W1, 'W2': W2}
    _L0_ffn_all = _L0_ffn_setup()
    _L0_ffn_in = {k: v for k, v in _L0_ffn_all.items() if k in ('Wr', 'W1', 'W2')}
    del _L0_ffn_all
    return {'x': x, 'src': src, 'dst': dst, 'edge_weight': edge_weight, 'L0_gnn_W_gcn': _L0_gnn_in['W_gcn'], 'L0_gnn_b_gcn': _L0_gnn_in['b_gcn'], 'L0_gnn_W_fc': _L0_gnn_in['W_fc'], 'L0_gnn_b_fc': _L0_gnn_in['b_fc'], 'L0_ffn_Wr': _L0_ffn_in['Wr'], 'L0_ffn_W1': _L0_ffn_in['W1'], 'L0_ffn_W2': _L0_ffn_in['W2']}

def reference(x, src, dst, edge_weight, L0_gnn_W_gcn, L0_gnn_b_gcn, L0_gnn_W_fc, L0_gnn_b_fc, L0_ffn_Wr, L0_ffn_W1, L0_ffn_W2):
    import jax
    import jax.numpy as jnp

    def _L0_gnn_ref(inputs, edge_index, edge_attr, W_gcn, b_gcn, W_fc, b_fc):
        import jax, jax.numpy as jnp
        import numpy as np
        N = 12500
        E = 100000
        IN_FEATS = 512
        N_HIDDEN = 128
        x = inputs @ W_gcn
        src, dst = (edge_index[0], edge_index[1])
        msg = x[src] * edge_attr[:, None]
        h = jax.ops.segment_sum(msg, dst, num_segments=inputs.shape[0]) + b_gcn
        return h @ W_fc.T + b_fc

    def _L0_ffn_ref(x, Wr, W1, W2):
        import jax, jax.numpy as jnp
        import numpy as np
        B, T, D, F, E, TOP_K = (8, 512, 512, 256, 8, 2)

        def _moe_forward(x, Wr, W1, W2):
            b, t, d = x.shape
            e = Wr.shape[1]
            xf = x.reshape(-1, d)
            n = xf.shape[0]
            logits = xf @ Wr
            probs = jax.nn.softmax(logits, axis=-1)
            w, idx = jax.lax.top_k(probs, TOP_K)
            w = w.astype(xf.dtype)
            gates = jnp.zeros((n, e), xf.dtype).at[jnp.arange(n)[:, None], idx].add(w)

            def body(acc, expert):
                w1, w2, g = expert
                h = jax.nn.gelu(xf @ w1, approximate=False)
                return (acc + g[:, None] * (h @ w2), None)
            out, _ = jax.lax.scan(body, jnp.zeros_like(xf), (W1, W2, gates.T))
            return out.reshape(b, t, d)
        return _moe_forward(x, Wr, W1, W2)
    edge_index = jnp.stack([src, dst])
    x = x + _L0_gnn_ref(_layernorm(x, axis=-1), edge_index, edge_weight, L0_gnn_W_gcn, L0_gnn_b_gcn, L0_gnn_W_fc, L0_gnn_b_fc)
    x = x + _L0_ffn_ref(_layernorm(x, axis=-1)[None], L0_ffn_Wr, L0_ffn_W1, L0_ffn_W2)[0]
    return x

_drawn_inputs = setup_inputs


def setup_inputs(seed=0):
    import zlib

    import numpy as np

    out = dict(_drawn_inputs(seed))
    spreads = {'L0_gnn_b_gcn': (0.0, 0.297)}
    factors = {'L0_gnn_b_fc': 2.87}
    for name, (base, spread) in spreads.items():
        noise = np.random.default_rng([zlib.crc32(name.encode()), seed]).standard_normal(out[name].shape)
        drawn = base * np.exp(spread * noise) if base else spread * noise
        out[name] = jnp.asarray(drawn.astype(out[name].dtype))
    for name, factor in factors.items():
        out[name] = (out[name] * factor).astype(out[name].dtype)
    return out
```

```python
from contextlib import ExitStack

import numpy as np

import concourse.bass as bass
from concourse import mybir

ALU = mybir.AluOpType
ACT = mybir.ActivationFunctionType
AX = mybir.AxisListType
F32 = mybir.dt.float32
F16 = mybir.dt.float16
BF16 = mybir.dt.bfloat16
I32 = mybir.dt.int32

P = 128
NODES, DIM, HID = 1250, 512, 128
EDGES = 41250
EXPERTS, FFN = 8, 256
EPS = 1e-5

KD = DIM // P
KF = FFN // P
TILES = -(-NODES // P)
LAST_ROWS = NODES - (TILES - 1) * P
PAD_NODES = TILES * P

GROUP = 16
GROUPS = 7
CHUNKS = 3
CT = GROUP * GROUPS
SPAN = P // GROUP
KEYS = TILES * SPAN
assert CT * CHUNKS * P >= EDGES and CT <= P
FULL_TILES = EDGES // P
REST = EDGES - FULL_TILES * P
LAST_FULL = FULL_TILES - 2 * CT
STEP = GROUP * P * NODES // EDGES
SLACK = 28
CHUNK_STEP = STEP * GROUPS
WINDOW = (GROUPS - 1) * STEP + P
assert WINDOW <= 512
HCOLS = (CHUNKS - 1) * CHUNK_STEP + WINDOW

NODE_TILES = [(0, 3), (3, 3), (6, 4)]
for _c, (_a, _n) in enumerate(NODE_TILES[:-1]):
    assert (_a + _n) * P <= (_c + 1) * CHUNK_STEP - SLACK
MAXT = max(n for _, n in NODE_TILES)

WS = 256.0
QUAD = 4
RING = 8

C_ID = 0
C_IOTA = C_ID + P
C_REP = C_IOTA + P
C_MASK = C_REP + P
C_START = C_MASK + GROUPS
C_DL = C_START + CHUNKS
C_LT = C_DL + 1
C_SEL = C_LT + EXPERTS * EXPERTS
NCONST = C_SEL + EXPERTS * P


def constants():
    c = np.zeros((P, NCONST), np.float32)
    p = np.arange(P)
    c[:, C_ID:C_ID + P] = np.eye(P)
    c[:, C_IOTA:C_IOTA + P] = p[None, :]
    c[:CT, C_REP:C_REP + P] = (p[:CT, None] % GROUP) == (p[None, :] // SPAN)
    c[:CT, C_MASK:C_MASK + GROUPS] = (p[:CT, None] // GROUP) == np.arange(GROUPS)[None, :]
    c[:CT, C_START:C_START + CHUNKS] = (p[:CT, None] // GROUP) * STEP + np.arange(CHUNKS)[None, :] * CHUNK_STEP - SLACK
    c[:, C_DL] = p % SPAN
    i = np.arange(EXPERTS)
    c[:, C_LT:C_LT + 64] = (i[None, :] < i[:, None]).astype(np.float32).reshape(1, 64)
    sel = (p[:3 * EXPERTS, None] % EXPERTS) == i[None, :]
    c[:3 * EXPERTS, C_SEL:] = np.repeat(sel, P, axis=1)
    return c


def gnn_moe_kernel(nc, x, src, dst, ew, w_gcn, b_gcn, w_fc, b_fc, w_r, w1, w2, const, out):
    ctx = ExitStack()
    with ctx:
        def sb(name, shape, dt=F32):
            return ctx.enter_context(nc.sbuf_tensor(name, shape, dt))

        def sem(name):
            return ctx.enter_context(nc.semaphore(name))

        cst = sb("cst", [P, NCONST])
        xs = sb("xs", [P, TILES, DIM])
        src_i = sb("src_i", [CT, CHUNKS, P], I32)
        dst_i = sb("dst_i", [CT, CHUNKS, P], I32)
        w_row = sb("w_row", [CT, CHUNKS, P])
        lo_i = sb("lo_i", [CT, CHUNKS, P], I32)
        hi_i = sb("hi_i", [CT, CHUNKS, P], I32)
        dl = sb("dl", [CT, CHUNKS, P])
        rel = sb("rel", [CT, CHUNKS, P])
        clip = sb("clip", [CT, CHUNKS, P])
        ok_span = sb("ok_span", [CT, CHUNKS, P])
        ok_win = sb("ok_win", [CT, CHUNKS, P])
        ROW_KEY, ROW_LO, ROW_W = range(3)
        rows = sb("rows", [CT, 3, CHUNKS, P])
        w_slow = sb("w_slow", [CT, CHUNKS, P])
        start_rel = sb("start_rel", [CT, CHUNKS])
        start_sel = sb("start_sel", [CT, CHUNKS, GROUPS])
        bad = sb("bad", [P, 1])
        bad_row = sb("bad_row", [1, 2])
        flag = sb("flag", [1, 1], I32)
        NSC = 5
        edge_sc = sb("edge_sc", [P, NSC, CHUNKS * CT])
        w_hi16 = sb("w_hi16", [P, 2, CT], BF16)
        group_sc = sb("group_sc", [P, NSC, GROUP])
        dval = sb("dval", [P, CHUNKS * GROUPS])
        iota_b = sb("iota_b", [P, P], BF16)
        one_src = sb("one_src", [P, RING, P], BF16)
        one_key = sb("one_key", [P, RING, 3, KEYS], BF16)
        adj = sb("adj", [P, TILES, GROUP * SPAN])
        part_h = sb("part_h", [P, HID])
        one_dst = sb("one_dst", [P, P])
        hT = sb("hT", [P, HCOLS])
        wg = sb("wg", [P, KD, HID])
        wfc = sb("wfc", [P, KD, HID])
        wfcT = sb("wfcT", [P, DIM])
        bg = sb("bg", [P, 1])
        bfc = sb("bfc", [1, DIM])
        wr = sb("wr", [P, KD, EXPERTS])
        wr_h = sb("wr_h", [P, 2, KD, EXPERTS], F16)
        xg = sb("xg", [P, TILES, HID])
        stats = sb("stats", [P, 6])
        mv = sb("mv", [P, MAXT, 2])
        std = sb("std", [P, MAXT])
        rstd = sb("rstd", [P, MAXT])
        nmr = sb("nmr", [P, MAXT])
        xn = sb("xn", [P, 2, DIM])
        xT = sb("xT", [P, KD, P])
        xT_h = sb("xT_h", [P, 2, KD, MAXT * P], F16)
        stage = sb("stage", [P, 2, KD * FFN])
        w1_h = sb("w1_h", [P, EXPERTS, 2, KD, FFN], F16)
        w2_h = sb("w2_h", [P, EXPERTS, 2, KF, DIM], F16)
        sel_b = sb("sel_b", [3 * EXPERTS, EXPERTS * P], BF16)
        lg = sb("lg", [P, MAXT, EXPERTS])
        mx = sb("mx", [P, MAXT])
        pr = sb("pr", [P, MAXT, EXPERTS])
        sm = sb("sm", [P, MAXT])
        cmp_gt = sb("cmp_gt", [P, MAXT, EXPERTS, EXPERTS])
        cmp_eq = sb("cmp_eq", [P, MAXT, EXPERTS, EXPERTS])
        rank = sb("rank", [P, MAXT, EXPERTS])
        g_b = sb("g_b", [P, 3, MAXT, EXPERTS], BF16)
        g_f = sb("g_f", [P, MAXT, 3, EXPERTS])
        gT = sb("gT", [3 * EXPERTS, MAXT * P], BF16)
        moe_f = sb("moe_f", [P, 2, KF, MAXT * P])
        act_o = moe_f[:, 0, :, :]
        hg = moe_f[:, 1, :, :]
        hg_h = sb("hg_h", [P, 2, KF, MAXT * P], F16)
        res = sb("res", [P, 2, DIM])

        ident = cst[:, C_ID:C_ID + P]
        iota = cst[:, C_IOTA:C_IOTA + P]

        bank = [ctx.enter_context(nc.psum_tensor(f"bank{i}", [P, 512], F32)) for i in range(8)]
        Y = bank[0:4]
        HPRE = bank[4:6]
        ADJ = bank[0:2]
        MIX = bank[6]
        HT = bank[7]

        s_const, s_edges, s_x, s_w = sem("const_in"), sem("edges_in"), sem("x_in"), sem("w_in")
        s_out = [sem("out_done0"), sem("out_done1")]
        s_pad = sem("pads_cleared")
        s_stage = [sem("stage_in0"), sem("stage_in1")]
        s_split = sem("expert_weights_split")
        s_scaled = sem("expert_weights_scaled")
        s_whi = sem("expert_weights_high")
        dv = sem("vector_step")
        ac = sem("scalar_step")
        s_rows = sem("edge_rows_ready")
        s_edgeT = sem("edge_rows_transposed")
        s_edgesc = sem("edge_scalars_ready")
        s_badT = sem("bad_transposed")
        s_flag = sem("flag_ready")
        s_dval = sem("window_rows_ready")
        s_mv = sem("norm_stats_ready")
        s_std = sem("norm_std_ready")
        s_rstd = sem("norm_scale_ready")
        s_xn = sem("normalised_ready")
        s_xnT = sem("normalised_transposed")
        s_xT = sem("transposed_copied")
        s_xg_ps = sem("xg_product")
        s_xg = sem("xg_ready")
        s_wfcT_ps = sem("wfc_transposed")
        s_wfcT = sem("wfc_ready")
        s_bfc_ps = sem("bfc_broadcast")
        s_xb = sem("x_plus_bias")
        s_one = sem("one_hots_ready")
        s_adj_ps = sem("adjacency_product")
        s_adj = sem("adjacency_copied")
        s_agg_ps = sem("aggregate_product")
        s_agg = sem("aggregate_copied")
        s_odst = sem("window_one_hot_ready")
        s_comb = sem("window_product")
        s_hT = sem("aggregate_added")
        s_fc = sem("fc_product")
        s_x2 = sem("x_plus_graph_layer")
        s_xh = sem("transposed_high")
        s_xl = sem("transposed_low")
        s_lg = sem("logits_product")
        s_sub = sem("logits_less_max")
        s_exp = sem("exp_ready")
        s_gf = sem("gates_ready")
        s_gT_ps = sem("gates_transposed")
        s_gT = sem("gates_rows_ready")
        s_gb = sem("gates_broadcast")
        s_h = sem("hidden_product")
        s_gelu = sem("gelu_ready")
        s_hg = sem("gated_ready")
        s_hh = sem("gated_high")
        s_hl = sem("gated_low")
        s_y = sem("expert_sum")
        s_res = sem("result_ready")
        s_prep = sem("constants_cast")
        s_slowT = sem("slow_transposed")
        s_slow_sc = sem("slow_scalars")
        s_slow_v = sem("slow_operand_ready")
        s_slow_p = sem("slow_product_ready")
        s_slow_add = sem("slow_added")
        s_slow_iota = sem("slow_iota")

        slow_sc = sb("slow_sc", [P, 3, CHUNKS * CT])
        slow_f = sb("slow_f", [CT, 2, CHUNKS, P])
        slow_gw = sb("slow_gw", [P, HID])
        slow_one = sb("slow_one", [P, PAD_NODES])
        slow_iota = adj[:, :, :].rearrange("p b n -> p (b n)")
        slow_turn = moe_f[:, :, :, :].rearrange("p a k n -> p (a k n)")[:, 0:PAD_NODES]
        block = ctx.enter_context(nc.Block())

        def edge_view(a, t0, n):
            return a[t0 * P:(t0 + n) * P].rearrange("(t e) -> t e", e=P)

        EDGE_DMAS = 3 * (CHUNKS + 1)
        W_DMAS = 5

        @block.sync
        def _(sp):
            sp.dma_start(cst[:, :], const[:, :]).then_inc(s_const, 16)
            sp.wait_ge(s_pad, 1)
            for a, t in ((src, src_i), (dst, dst_i), (ew, w_row)):
                for c in range(CHUNKS):
                    n = CT if c < CHUNKS - 1 else LAST_FULL
                    sp.dma_start(t[0:n, c, :], edge_view(a, c * CT, n)).then_inc(s_edges, 16)
                sp.dma_start(t[LAST_FULL:LAST_FULL + 1, CHUNKS - 1, 0:REST],
                             a[FULL_TILES * P:EDGES].rearrange("(t e) -> t e", t=1)).then_inc(s_edges, 16)
            sp.dma_start(wg[:, :, :], w_gcn.rearrange("(k p) h -> p k h", p=P)).then_inc(s_w, 16)
            sp.dma_start(wfc[:, :, :], w_fc.rearrange("(k p) h -> p k h", p=P)).then_inc(s_w, 16)
            sp.dma_start(bg[:, :], b_gcn.rearrange("(p a) -> p a", a=1)).then_inc(s_w, 16)
            sp.dma_start(bfc[:, :], b_fc.rearrange("(a n) -> a n", a=1)).then_inc(s_w, 16)
            sp.dma_start(wr[:, :, :], w_r.rearrange("(k p) e -> p k e", p=P)).then_inc(s_w, 16)
            for n in range(2 * EXPERTS):
                e = n // 2
                if n >= 2:
                    sp.wait_ge(s_split, n - 1)
                w = w1[e].rearrange("(k p) f -> p k f", p=P) if n % 2 == 0 else w2[e].rearrange("(k p) d -> p k d", p=P)
                sp.dma_start(stage[:, n % 2, :].rearrange("p (k f) -> p k f", k=KD if n % 2 == 0 else KF), w)\
                  .then_inc(s_stage[n % 2], 16)

        def results(eng):
            for t in range(TILES):
                eng.wait_ge(s_res, t + 1)
                r = P if t < TILES - 1 else LAST_ROWS
                eng.dma_start(out[t * P:t * P + r, :], res[0:r, t % 2, :]).then_inc(s_out[t % 2], 16)
            for i in range(2):
                eng.wait_ge(s_out[i], 16 * (TILES // 2))

        @block.gpsimd
        def _(pool):
            for t in (src_i, dst_i):
                pool.memset(t[96:CT, CHUNKS - 1, :], 0)
            pool.memset(w_row[96:CT, CHUNKS - 1, :], 0.0).then_inc(s_pad, 1)
            pool.memset(xs[96:P, TILES - 1, :], 0.0).then_inc(s_pad, 1)
            pool.wait_ge(s_pad, 2)
            for a, b in ((0, 3), (3, 6), (6, TILES - 1)):
                pool.dma_start(xs[:, a:b, :], x[a * P:b * P, :].rearrange("(t p) d -> p t d", p=P)).then_inc(s_x, 16)
            pool.dma_start(xs[0:LAST_ROWS, TILES - 1, :], x[(TILES - 1) * P:NODES, :]).then_inc(s_x, 16)
            for n in range(2 * EXPERTS):
                pool.wait_ge(s_stage[n % 2], 16 * (n // 2 + 1))
                pool.tensor_scalar(stage[:, n % 2, :], stage[:, n % 2, :], WS, None, ALU.mult).then_inc(s_scaled, 1)
                pool.wait_ge(s_scaled, n + 1)
                pool.wait_ge(s_whi, n + 1)
                dest = (w1_h if n % 2 == 0 else w2_h)[:, n // 2, :, :, :].rearrange("p s k f -> p s (k f)")
                pool.tensor_tensor(dest[:, 1, :], stage[:, n % 2, :], dest[:, 0, :], ALU.subtract).then_inc(s_split, 1)
            results(pool)

        @block.scalar
        def _(act):
            def split_high(n):
                act.wait_ge(s_scaled, n + 1)
                dest = (w1_h if n % 2 == 0 else w2_h)[:, n // 2, :, :, :].rearrange("p s k f -> p s (k f)")
                act.activation(dest[:, 0, :], stage[:, n % 2, :], ACT.Copy).then_inc(s_whi, 1)

            for t in range(TILES):
                act.wait_ge(s_mv, t + 1)
                act.activation(std[:, t % MAXT:t % MAXT + 1], mv[:, t % MAXT, 1:2], ACT.Sqrt).then_inc(s_std, 1)
                act.wait_ge(s_rstd, t + 1)
                if t >= 2:
                    act.wait_ge(s_xnT, t - 1)
                act.activation(xn[:, t % 2, :], xs[:, t, :], ACT.Identity, bias=nmr[:, t % MAXT:t % MAXT + 1],
                               scale=rstd[:, t % MAXT:t % MAXT + 1]).then_inc(s_xn, 1)
                act.wait_ge(s_xnT, t + 1)
                if t >= 1:
                    act.wait_ge(s_xg_ps, t)
                act.activation(xT[:, :, :], bank[t % 2][:, :].rearrange("p (k n) -> p k n", k=KD), ACT.Copy)\
                   .then_inc(s_xT, 1)
                act.wait_ge(s_xg_ps, t + 1)
                act.activation(xg[:, t, :], bank[2 + t % 2][:, 0:HID], ACT.Copy).then_inc(s_xg, 1)
            for n in range(2 * EXPERTS):
                split_high(n)

            def edge_group(c, j):
                g = c * GROUPS + j
                for i in range(GROUP // QUAD):
                    act.wait_ge(s_adj_ps, g * (GROUP // QUAD) + i + 1)
                    o = adj[:, :, QUAD * i * SPAN:QUAD * (i + 1) * SPAN].rearrange("p b (t s) -> p t b s", t=QUAD)
                    act.activation(o, ADJ[i % 2][:, 0:QUAD * KEYS].rearrange("p (t b s) -> p t b s", t=QUAD, s=SPAN),
                                   ACT.Copy).then_inc(s_adj, 1)
                act.wait_ge(s_agg_ps, g + 1)
                act.activation(part_h[:, :], MIX[:, 0:HID], ACT.Copy).then_inc(s_agg, 1)

            def prepare(c):
                a, n = NODE_TILES[c]
                for t in range(a, a + n):
                    act.wait_ge(s_mv, TILES + t + 1)
                    act.activation(std[:, t - a:t - a + 1], mv[:, t - a, 1:2], ACT.Sqrt).then_inc(s_std, 1)
                    act.wait_ge(s_rstd, TILES + t + 1)
                    act.wait_ge(s_xnT, TILES + t - 1)
                    act.activation(xn[:, t % 2, :], xs[:, t, :], ACT.Identity, bias=nmr[:, t - a:t - a + 1],
                                   scale=rstd[:, t - a:t - a + 1]).then_inc(s_xn, 1)
                    act.wait_ge(s_xnT, TILES + t + 1)
                    act.activation(xT_h[:, 0, :, (t - a) * P:(t - a + 1) * P],
                                   HPRE[t % 2][:, :].rearrange("p (k n) -> p k n", k=KD), ACT.Copy).then_inc(s_xh, 1)
                act.wait_ge(s_sub, c + 1)
                act.activation(pr[:, 0:n, :], lg[:, 0:n, :], ACT.Exp).then_inc(s_exp, 1)

            def expert(c, e):
                a, n = NODE_TILES[c]
                w = n * P
                for f in range(KF):
                    k = (c * EXPERTS + e) * KF + f
                    act.wait_ge(s_h, k + 1)
                    if k >= KF:
                        act.wait_ge(s_hg, k - KF + 1)
                    act.activation(act_o[:, f, 0:w], HPRE[f][:, 0:w], ACT.Gelu, scale=1.0 / WS).then_inc(s_gelu, 1)
                    act.wait_ge(s_hg, k + 1)
                    if k >= KF:
                        act.wait_ge(s_y, c * EXPERTS + e)
                    act.activation(hg_h[:, 0, f, 0:w], hg[:, f, 0:w], ACT.Copy).then_inc(s_hh, 1)

            for c in range(CHUNKS):
                for j in range(GROUPS):
                    edge_group(c, j)
                prepare(c)
                for e in range(EXPERTS):
                    expert(c, e)

        @block.vector
        def _(dve):
            steps = [0]

            def step(ins):
                steps[0] += 1
                ins.then_inc(dv, 1)
                dve.wait_ge(dv, steps[0])

            dve.wait_ge(s_edges, 16 * EDGE_DMAS)
            dve.wait_ge(s_const, 16)
            dve.wait_ge(s_pad, 1)
            dve.tensor_scalar(lo_i[:, :, :], src_i[:, :, :], P - 1, None, ALU.bitwise_and)
            dve.tensor_scalar(hi_i[:, :, :], src_i[:, :, :], 7, None, ALU.logical_shift_right)
            dve.tensor_tensor(dl[:, :, :], dst_i[:, :, :], dst_i[:, :, 0:1].broadcast_to([CT, CHUNKS, P]), ALU.subtract)
            starts = cst[0:CT, C_START:C_START + CHUNKS]
            dve.tensor_tensor(rel[:, :, :], dst_i[:, :, :],
                              starts.rearrange("p (c o) -> p c o", o=1).broadcast_to([CT, CHUNKS, P]), ALU.subtract)
            step(dve.tensor_tensor(start_rel[:, :], dst_i[:, :, 0], starts, ALU.subtract))
            dve.tensor_copy(rows[:, ROW_LO, :, :], lo_i[:, :, :])
            dve.scalar_tensor_tensor(out=rows[:, ROW_KEY, :, :], in0=hi_i[:, :, :], scalar=float(SPAN),
                                     in1=dl[:, :, :], op0=ALU.mult, op1=ALU.add)
            step(dve.tensor_scalar(clip[:, :, :], dl[:, :, :], 0.0, float(SPAN - 1), ALU.max, ALU.min))
            step(dve.tensor_tensor(ok_span[:, :, :], clip[:, :, :], dl[:, :, :], ALU.is_equal))
            step(dve.tensor_scalar(clip[:, :, :], rel[:, :, :], 0.0, float(P - 1), ALU.max, ALU.min))
            step(dve.tensor_tensor(ok_win[:, :, :], clip[:, :, :], rel[:, :, :], ALU.is_equal))
            step(dve.tensor_tensor(ok_span[:, :, :], ok_span[:, :, :], ok_win[:, :, :], ALU.mult))
            step(dve.tensor_tensor(rows[:, ROW_W, :, :], w_row[:, :, :], ok_span[:, :, :], ALU.mult))
            dve.tensor_tensor(start_sel[:, :, :],
                              start_rel[:, :].rearrange("p (c o) -> p c o", o=1).broadcast_to([CT, CHUNKS, GROUPS]),
                              cst[0:CT, C_MASK:C_MASK + GROUPS].rearrange("p (o j) -> p o j", o=1)
                              .broadcast_to([CT, CHUNKS, GROUPS]), ALU.mult)
            dve.memset(bad[:, :], 0.0)
            step(dve.tensor_tensor(w_slow[:, :, :], w_row[:, :, :], rows[:, ROW_W, :, :], ALU.subtract))
            dve.tensor_reduce(bad[0:CT, :], w_slow[:, :, :], AX.XY, ALU.max, apply_absolute_value=True)\
               .then_inc(s_rows, 1)
            dve.tensor_copy(iota_b[:, :], iota)
            dve.tensor_copy(sel_b[:, :], cst[0:3 * EXPERTS, C_SEL:C_SEL + EXPERTS * P])
            dve.wait_ge(s_w, 16 * W_DMAS)
            step(dve.tensor_scalar(wr_h[:, 0, :, :], wr[:, :, :], WS, None, ALU.mult))
            dve.scalar_tensor_tensor(out=wr_h[:, 1, :, :], in0=wr[:, :, :], scalar=WS, in1=wr_h[:, 0, :, :],
                                     op0=ALU.mult, op1=ALU.subtract)
            step(dve.memset(hT[:, :], 0.0))
            dve.tensor_scalar(hT[:, :], hT[:, :], bg[:, 0:1], None, ALU.add).then_inc(s_prep, 1)
            dve.wait_ge(s_badT, 1)
            step(dve.tensor_reduce(bad_row[:, 0:1], bank[6][0:1, 0:P], AX.X, ALU.max))
            step(dve.tensor_scalar(bad_row[:, 1:2], bad_row[:, 0:1], 0.0, None, ALU.is_gt))
            dve.tensor_copy(flag[:, :], bad_row[:, 1:2]).then_inc(s_flag, 1)
            dve.wait_ge(s_edgeT, CHUNKS + 1)
            dve.tensor_scalar(dval[:, :], bank[7][:, 0:CHUNKS * GROUPS], cst[:, C_DL:C_DL + 1], None, ALU.add)\
               .then_inc(s_dval, 1)
            for c in range(CHUNKS):
                col = slice(c * CT, (c + 1) * CT)
                step(dve.tensor_copy(edge_sc[:, 0:3, col],
                                     bank[3 + c][:, 0:3 * CT].rearrange("p (a t) -> p a t", a=3)))
                step(dve.tensor_copy(w_hi16[:, 0, :], edge_sc[:, 2, col]))
                step(dve.tensor_tensor(edge_sc[:, 3, col], edge_sc[:, 2, col], w_hi16[:, 0, :], ALU.subtract))
                step(dve.tensor_copy(w_hi16[:, 1, :], edge_sc[:, 3, col]))
                dve.tensor_tensor(edge_sc[:, 4, col], edge_sc[:, 3, col], w_hi16[:, 1, :], ALU.subtract)\
                   .then_inc(s_edgesc, 1)

            def norm_stats(t, slot, xt):
                step(dve.bn_stats(stats[:, :], xt))
                step(dve.bn_aggr(mv[:, slot, :], stats[:, :]))
                dve.tensor_scalar(mv[:, slot, 1:2], mv[:, slot, 1:2], EPS, None, ALU.add).then_inc(s_mv, 1)
                dve.wait_ge(s_std, t + 1)
                step(dve.reciprocal(rstd[:, slot:slot + 1], std[:, slot:slot + 1]))
                dve.scalar_tensor_tensor(out=nmr[:, slot:slot + 1], in0=mv[:, slot, 0:1], scalar=-1.0,
                                         in1=rstd[:, slot:slot + 1], op0=ALU.mult, op1=ALU.mult).then_inc(s_rstd, 1)

            dve.wait_ge(s_x, 64)
            for t in range(TILES):
                if t >= MAXT:
                    dve.wait_ge(s_xn, t - MAXT + 1)
                norm_stats(t, t % MAXT, xs[:, t, :])
            dve.wait_ge(s_bfc_ps, 1)
            dve.wait_ge(s_xn, TILES)
            for t in range(TILES):
                dve.tensor_tensor(xs[:, t, :], xs[:, t, :], bank[7][:, :], ALU.add).then_inc(s_xb, 1)
            dve.wait_ge(s_wfcT_ps, 1)
            dve.tensor_copy(wfcT[:, :], bank[6][:, :]).then_inc(s_wfcT, 1)

            slow = dve.value_load(flag[0:1, 0:1], min_val=0, max_val=1)
            with dve.If(slow > 0):
                dve.tensor_copy(slow_f[:, 0, :, :], src_i[:, :, :])
                dve.tensor_copy(slow_f[:, 1, :, :], dst_i[:, :, :]).then_inc(s_slow_sc, 1)
                dve.wait_ge(s_slowT, 1)
                for c in range(CHUNKS):
                    dve.tensor_copy(slow_sc[:, :, c * CT:(c + 1) * CT],
                                    bank[c][:, 0:3 * CT].rearrange("p (a t) -> p a t", a=3)).then_inc(s_slow_sc, 1)
                dve.wait_ge(s_slow_sc, 1 + CHUNKS)
                for b in range(TILES):
                    ins = dve.tensor_scalar(slow_iota[:, b * P:(b + 1) * P], iota, float(b * P), None, ALU.add)
                ins.then_inc(s_slow_iota, 1)
                dve.wait_ge(s_slow_iota, 1)
                with dve.Fori(0, FULL_TILES + 1) as t:
                    dve.tensor_scalar(slow_one[:, :], slow_iota, slow_sc[:, 0, bass.ds(t, 1)], None,
                                      ALU.is_equal).then_inc(s_slow_v, 1)
                    dve.wait_ge(s_slow_p, t * 3 + 1)
                    for b in range(3):
                        w = min(512, PAD_NODES - 512 * b)
                        dve.tensor_copy(slow_turn[:, 512 * b:512 * b + w], bank[3 + b][:, 0:w])
                    dve.tensor_scalar(slow_one[:, :], slow_iota, slow_sc[:, 1, bass.ds(t, 1)], None,
                                      ALU.is_equal).then_inc(s_slow_v, 1)
                    dve.wait_ge(s_slow_p, t * 3 + 2)
                    dve.tensor_scalar(slow_gw[:, :], bank[2][:, 0:HID], slow_sc[:, 2, bass.ds(t, 1)], None,
                                      ALU.mult).then_inc(s_slow_v, 1)
                    dve.wait_ge(s_slow_p, t * 3 + 3)
                    for b in range(3):
                        w = min(512, PAD_NODES - 512 * b)
                        ins = dve.tensor_tensor(hT[:, SLACK + 512 * b:SLACK + 512 * b + w], bank[3 + b][:, 0:w],
                                                hT[:, SLACK + 512 * b:SLACK + 512 * b + w], ALU.add)
                    ins.then_inc(s_slow_add, 1)
                    dve.wait_ge(s_slow_add, t + 1)
            dve.end_ifs()

            def edge_group(c, j):
                g = c * GROUPS + j
                if j == 0:
                    dve.wait_ge(s_edgesc, c + 1)
                if g:
                    dve.wait_ge(s_one, g * GROUP)
                step(dve.tensor_copy(group_sc[:, :, :],
                                     edge_sc[:, :, g * GROUP:(g + 1) * GROUP]))
                for i in range(GROUP):
                    t = g * GROUP + i
                    if t >= RING:
                        dve.wait_ge(s_adj_ps, (t - RING) // QUAD + 1)
                    r = i % RING
                    dve.tensor_scalar(one_src[:, r, :], iota_b[:, :], group_sc[:, 1, i:i + 1], None, ALU.is_equal)
                    for k in range(3):
                        ins = dve.tensor_scalar(one_key[:, r, k, :], iota_b[:, 0:KEYS], group_sc[:, 0, i:i + 1],
                                                group_sc[:, 2 + k, i:i + 1], ALU.is_equal, ALU.mult)
                    ins.then_inc(s_one, 1)
                if g >= 1:
                    dve.wait_ge(s_comb, g)
                dve.tensor_scalar(one_dst[:, :], iota, dval[:, g:g + 1], None, ALU.is_equal).then_inc(s_odst, 1)

            def add_chunk(c):
                dve.wait_ge(s_comb, (c + 1) * GROUPS)
                cols = slice(c * CHUNK_STEP, c * CHUNK_STEP + WINDOW)
                dve.tensor_tensor(hT[:, cols], HT[:, 0:WINDOW], hT[:, cols], ALU.add).then_inc(s_hT, 1)
                dve.wait_ge(s_hT, c + 1)

            def prepare(c):
                a, n = NODE_TILES[c]
                for t in range(a, a + n):
                    dve.wait_ge(s_fc, t + 1)
                    step(dve.tensor_tensor(xs[:, t, :], Y[t % 2][:, :], xs[:, t, :], ALU.add))
                    norm_stats(TILES + t, t - a, xs[:, t, :])
                    dve.wait_ge(s_xh, t + 1)
                    dve.tensor_tensor(xT_h[:, 1, :, (t - a) * P:(t - a + 1) * P],
                                      HPRE[t % 2][:, :].rearrange("p (k n) -> p k n", k=KD),
                                      xT_h[:, 0, :, (t - a) * P:(t - a + 1) * P], ALU.subtract).then_inc(s_xl, 1)
                dve.wait_ge(s_lg, c + 1)

                def along(t2, inner):
                    return t2.rearrange("p (n o) -> p n o", o=1).broadcast_to([P, n, inner])

                L = MIX[:, 0:n * EXPERTS].rearrange("p (n e) -> p n e", n=n)
                step(dve.tensor_reduce(mx[:, 0:n], L, AX.X, ALU.max))
                step(dve.tensor_tensor(lg[:, 0:n, :], L, along(mx[:, 0:n], EXPERTS), ALU.subtract))
                dve.tensor_scalar(lg[:, 0:n, :], lg[:, 0:n, :], 1.0 / WS, None, ALU.mult).then_inc(s_sub, 1)
                dve.wait_ge(s_exp, c + 1)
                step(dve.tensor_reduce(sm[:, 0:n], pr[:, 0:n, :], AX.X, ALU.add))
                step(dve.reciprocal(sm[:, 0:n], sm[:, 0:n]))
                step(dve.tensor_tensor(pr[:, 0:n, :], pr[:, 0:n, :], along(sm[:, 0:n], EXPERTS), ALU.mult))
                pj = pr[:, 0:n, :].rearrange("p n (o j) -> p n o j", o=1).broadcast_to([P, n, EXPERTS, EXPERTS])
                pi = pr[:, 0:n, :].rearrange("p n (i o) -> p n i o", o=1).broadcast_to([P, n, EXPERTS, EXPERTS])
                lt = cst[:, C_LT:C_LT + 64].rearrange("p (o i j) -> p o i j", o=1, i=EXPERTS)\
                    .broadcast_to([P, n, EXPERTS, EXPERTS])
                dve.tensor_tensor(cmp_gt[:, 0:n, :, :], pj, pi, ALU.is_gt)
                step(dve.tensor_tensor(cmp_eq[:, 0:n, :, :], pj, pi, ALU.is_equal))
                step(dve.tensor_tensor(cmp_eq[:, 0:n, :, :], cmp_eq[:, 0:n, :, :], lt, ALU.mult))
                step(dve.tensor_tensor(cmp_gt[:, 0:n, :, :], cmp_gt[:, 0:n, :, :], cmp_eq[:, 0:n, :, :], ALU.add))
                step(dve.tensor_reduce(rank[:, 0:n, :], cmp_gt[:, 0:n, :, :], AX.X, ALU.add))
                step(dve.tensor_scalar(rank[:, 0:n, :], rank[:, 0:n, :], 1.5, None, ALU.is_lt))
                step(dve.tensor_tensor(pr[:, 0:n, :], pr[:, 0:n, :], rank[:, 0:n, :], ALU.mult))
                for k in range(3):
                    step(dve.tensor_copy(g_b[:, k, 0:n, :], pr[:, 0:n, :]))
                    if k == 0 and c:
                        dve.wait_ge(s_gT_ps, c)
                    ins = dve.tensor_copy(g_f[:, 0:n, k, :], g_b[:, k, 0:n, :])
                    if k < 2:
                        step(dve.tensor_tensor(pr[:, 0:n, :], pr[:, 0:n, :], g_b[:, k, 0:n, :], ALU.subtract))
                ins.then_inc(s_gf, 1)
                dve.wait_ge(s_gT_ps, c + 1)
                dve.tensor_copy(gT[:, 0:n * P], HT[0:3 * EXPERTS, 0:n * P]).then_inc(s_gT, 1)

            def expert(c, e):
                a, n = NODE_TILES[c]
                w = n * P
                G = Y[3] if n < MAXT else MIX
                for f in range(KF):
                    k = (c * EXPERTS + e) * KF + f
                    dve.wait_ge(s_gelu, k + 1)
                    dve.wait_ge(s_gb, c * EXPERTS + e + 1)
                    if k >= KF:
                        dve.wait_ge(s_hh, k - KF + 1)
                        dve.wait_ge(s_hl, k - KF + 1)
                    dve.tensor_tensor(hg[:, f, 0:w], act_o[:, f, 0:w], G[:, 0:w], ALU.mult).then_inc(s_hg, 1)
                for f in range(KF):
                    k = (c * EXPERTS + e) * KF + f
                    dve.wait_ge(s_hh, k + 1)
                    dve.tensor_tensor(hg_h[:, 1, f, 0:w], hg[:, f, 0:w], hg_h[:, 0, f, 0:w],
                                      ALU.subtract).then_inc(s_hl, 1)

            def finish(c):
                a, n = NODE_TILES[c]
                dve.wait_ge(s_y, (c + 1) * EXPERTS)
                for t in range(a, a + n):
                    if t >= 2:
                        dve.wait_ge(s_out[t % 2], 16 * (t // 2))
                    dve.scalar_tensor_tensor(out=res[:, t % 2, :], in0=Y[t - a][:, :], scalar=1.0 / WS,
                                             in1=xs[:, t, :], op0=ALU.mult, op1=ALU.add).then_inc(s_res, 1)

            for c in range(CHUNKS):
                for j in range(GROUPS):
                    edge_group(c, j)
                add_chunk(c)
                prepare(c)
                for e in range(EXPERTS):
                    expert(c, e)
                finish(c)

        @block.tensor
        def _(pe):
            pe.wait_ge(s_const, 16)
            pe.wait_ge(s_rows, 1)
            pe.transpose(bank[6][0:1, 0:P], bad[:, 0:1], ident).then_inc(s_badT, 1)
            for c in range(CHUNKS):
                for a in range(3):
                    ins = pe.transpose(bank[3 + c][:, a * CT:(a + 1) * CT], rows[:, a, c, :], cst[0:CT, C_ID:C_ID + CT])
                ins.then_inc(s_edgeT, 1)
            pe.matmul(bank[7][:, 0:CHUNKS * GROUPS], cst[0:CT, C_REP:C_REP + P],
                      start_sel[:, :, :].rearrange("p c j -> p (c j)"), start=True, stop=True).then_inc(s_edgeT, 1)
            pe.wait_ge(s_w, 16 * W_DMAS)
            for t in range(TILES):
                pe.wait_ge(s_xn, t + 1)
                if t >= 2:
                    pe.wait_ge(s_xT, t - 1)
                for k in range(KD):
                    ins = pe.transpose(bank[t % 2][:, k * P:(k + 1) * P], xn[:, t % 2, k * P:(k + 1) * P], ident)
                ins.then_inc(s_xnT, 1)
                pe.wait_ge(s_xT, t + 1)
                if t >= 2:
                    pe.wait_ge(s_xg, t - 1)
                if t == 1:
                    pe.wait_ge(s_edgesc, 1)
                for k in range(KD):
                    ins = pe.matmul(bank[2 + t % 2][:, 0:HID], xT[:, k, :], wg[:, k, :], start=(k == 0), stop=(k == KD - 1))
                ins.then_inc(s_xg_ps, 1)
            pe.wait_ge(s_dval, 1)
            pe.matmul(bank[7][:, :], ones_row(cst), bfc[:, :],
                      start=True, stop=True).then_inc(s_bfc_ps, 1)
            pe.wait_ge(s_flag, 1)
            for k in range(KD):
                ins = pe.transpose(bank[6][:, k * P:(k + 1) * P], wfc[:, k, :], ident)
            ins.then_inc(s_wfcT_ps, 1)

            slow = pe.value_load(flag[0:1, 0:1], min_val=0, max_val=1)
            with pe.If(slow > 0):
                pe.wait_ge(s_slow_sc, 1)
                pe.wait_ge(s_xg, TILES)
                for c in range(CHUNKS):
                    for a in range(3):
                        row = slow_f[:, a, c, :] if a < 2 else w_slow[:, c, :]
                        ins = pe.transpose(bank[c][:, a * CT:(a + 1) * CT], row, cst[0:CT, C_ID:C_ID + CT])
                ins.then_inc(s_slowT, 1)
                pe.wait_ge(s_slow_sc, 1 + CHUNKS)
                with pe.Fori(0, FULL_TILES + 1) as t:
                    pe.wait_ge(s_slow_v, t * 3 + 1)
                    for b in range(TILES):
                        ins = pe.transpose(bank[3 + b // 4][:, (b % 4) * P:(b % 4 + 1) * P],
                                           slow_one[:, b * P:(b + 1) * P], ident)
                    ins.then_inc(s_slow_p, 1)
                    pe.wait_ge(s_slow_v, t * 3 + 2)
                    for b in range(TILES):
                        ins = pe.matmul(bank[2][:, 0:HID], slow_turn[:, b * P:(b + 1) * P], xg[:, b, :],
                                        start=(b == 0), stop=(b == TILES - 1))
                    ins.then_inc(s_slow_p, 1)
                    pe.wait_ge(s_slow_v, t * 3 + 3)
                    for b in range(3):
                        w = min(512, PAD_NODES - 512 * b)
                        ins = pe.matmul(bank[3 + b][:, 0:w], slow_gw[:, :], slow_one[:, 512 * b:512 * b + w],
                                        start=True, stop=True)
                    ins.then_inc(s_slow_p, 1)
                pe.wait_ge(s_slow_add, FULL_TILES + 1)
            pe.end_ifs()
            pe.wait_ge(s_xg, TILES)
            pe.wait_ge(s_wfcT, 1)
            pe.wait_ge(s_xb, TILES)
            pe.wait_ge(s_prep, 1)

            def edge_group(c, j):
                g = c * GROUPS + j
                for i in range(GROUP):
                    t = g * GROUP + i
                    pe.wait_ge(s_one, t + 1)
                    if i % QUAD == 0 and t >= 2 * QUAD:
                        pe.wait_ge(s_adj, t // QUAD - 1)
                    o = ADJ[i // QUAD % 2][:, i % QUAD * KEYS:(i % QUAD + 1) * KEYS]
                    for k in range(3):
                        ins = pe.matmul(o, one_src[:, i % RING, :], one_key[:, i % RING, k, :],
                                        start=(k == 0), stop=(k == 2))
                    if i % QUAD == QUAD - 1:
                        ins.then_inc(s_adj_ps, 1)
                pe.wait_ge(s_adj, (g + 1) * (GROUP // QUAD))
                if g >= 1:
                    pe.wait_ge(s_agg, g)
                for b in range(TILES):
                    ins = pe.matmul(MIX[:, 0:HID], adj[:, b, :], xg[:, b, :], start=(b == 0), stop=(b == TILES - 1))
                ins.then_inc(s_agg_ps, 1)
                pe.wait_ge(s_agg, g + 1)
                pe.wait_ge(s_odst, g + 1)
                pe.matmul(HT[:, j * STEP:j * STEP + P], part_h[:, :], one_dst[:, :], start=(j == 0),
                          stop=(j == GROUPS - 1), skip_group_check=True).then_inc(s_comb, 1)

            def prepare(c):
                a, n = NODE_TILES[c]
                pe.wait_ge(s_hT, c + 1)
                if c:
                    pe.wait_ge(s_res, a)
                for t in range(a, a + n):
                    if t >= a + 2:
                        pe.wait_ge(s_xl, t - 1)
                    pe.matmul(Y[t % 2][:, :], hT[:, SLACK + t * P:SLACK + (t + 1) * P], wfcT[:, :],
                              start=True, stop=True).then_inc(s_fc, 1)
                    pe.wait_ge(s_xn, TILES + t + 1)
                    if t >= a + 2:
                        pe.wait_ge(s_xh, t - 1)
                    for k in range(KD):
                        ins = pe.transpose(HPRE[t % 2][:, k * P:(k + 1) * P], xn[:, t % 2, k * P:(k + 1) * P], ident)
                    ins.then_inc(s_xnT, 1)
                pe.wait_ge(s_xl, a + n)
                for t in range(n):
                    terms = [(x_h, w_h, k) for x_h, w_h in ((0, 0), (0, 1), (1, 0)) for k in range(KD)]
                    for m, (x_h, w_h, k) in enumerate(terms):
                        ins = pe.matmul(MIX[:, t * EXPERTS:(t + 1) * EXPERTS], xT_h[:, x_h, k, t * P:(t + 1) * P],
                                        wr_h[:, w_h, k, :], start=(m == 0), stop=(m == len(terms) - 1))
                ins.then_inc(s_lg, 1)
                pe.wait_ge(s_gf, c + 1)
                for t in range(n):
                    ins = pe.transpose(HT[0:3 * EXPERTS, t * P:(t + 1) * P],
                                       g_f[:, t, :, :].rearrange("p k e -> p (k e)"), ident)
                ins.then_inc(s_gT_ps, 1)
                pe.wait_ge(s_gT, c + 1)

            def expert(c, e):
                a, n = NODE_TILES[c]
                w = n * P
                G = Y[3] if n < MAXT else MIX
                q = c * EXPERTS + e
                if q:
                    pe.wait_ge(s_hg, q * KF)
                pe.matmul(G[:, 0:w], sel_b[:, e * P:(e + 1) * P], gT[:, 0:w], start=True, stop=True).then_inc(s_gb, 1)
                for f in range(KF):
                    if q:
                        pe.wait_ge(s_gelu, (q - 1) * KF + f + 1)
                    terms = [(w_h, x_h, k) for w_h, x_h in ((0, 0), (0, 1), (1, 0)) for k in range(KD)]
                    for m, (w_h, x_h, k) in enumerate(terms):
                        ins = pe.matmul(HPRE[f][:, 0:w], w1_h[:, e, w_h, k, f * P:(f + 1) * P], xT_h[:, x_h, k, 0:w],
                                        start=(m == 0), stop=(m == len(terms) - 1))
                    ins.then_inc(s_h, 1)
                pe.wait_ge(s_hl, (q + 1) * KF)
                pe.wait_ge(s_hh, (q + 1) * KF)
                for t in range(n):
                    terms = [(h_h, w_h, k) for k in range(KF) for h_h, w_h in ((0, 0), (0, 1), (1, 0))]
                    for m, (h_h, w_h, k) in enumerate(terms):
                        ins = pe.matmul(Y[t][:, :], hg_h[:, h_h, k, t * P:(t + 1) * P], w2_h[:, e, w_h, k, :],
                                        start=(e == 0 and m == 0), stop=(e == EXPERTS - 1 and m == len(terms) - 1),
                                        skip_group_check=True)
                ins.then_inc(s_y, 1)

            for c in range(CHUNKS):
                if c:
                    pe.wait_ge(s_res, NODE_TILES[c][0])
                for j in range(GROUPS):
                    edge_group(c, j)
                prepare(c)
                if c == 0:
                    pe.wait_ge(s_split, 2 * EXPERTS)
                for e in range(EXPERTS):
                    expert(c, e)


def ones_row(cst):
    return cst[0:1, C_SEL:C_SEL + P]


_INS = ["x", "src", "dst", "edge_weight", "L0_gnn_W_gcn", "L0_gnn_b_gcn", "L0_gnn_W_fc", "L0_gnn_b_fc",
        "L0_ffn_Wr", "L0_ffn_W1", "L0_ffn_W2"]


def kernel(**inputs):
    import concourse.bacc as bacc
    from concourse.bass_utils import run_bass_kernel_spmd

    nc = bacc.Bacc("TRN2", target_bir_lowering=False, num_devices=1)
    arrays, args = {}, []
    for name in _INS:
        a = np.ascontiguousarray(inputs[name])
        arrays[f"in_{name}"] = a
        args.append(nc.dram_tensor(f"in_{name}", a.shape, mybir.dt.from_np(a.dtype), kind="ExternalInput").ap())
    arrays["in_constants"] = constants()
    args.append(nc.dram_tensor("in_constants", (P, NCONST), F32, kind="ExternalInput").ap())
    out = nc.dram_tensor("out", (NODES, DIM), F32, kind="ExternalOutput").ap()
    gnn_moe_kernel(nc, *args, out)
    r = run_bass_kernel_spmd(nc, [arrays], core_ids=[0])
    return r.results[0]["out"]
```

```python
from contextlib import ExitStack

import numpy as np

import concourse.bass as bass
from concourse import mybir

ALU = mybir.AluOpType
ACT = mybir.ActivationFunctionType
AX = mybir.AxisListType
F32 = mybir.dt.float32
F16 = mybir.dt.float16
BF16 = mybir.dt.bfloat16
I32 = mybir.dt.int32

P = 128
NODES, DIM, HID = 1250, 512, 128
EDGES = 41250
EXPERTS, FFN = 8, 256
EPS = 1e-5

KD = DIM // P
KF = FFN // P
TILES = -(-NODES // P)
LAST_ROWS = NODES - (TILES - 1) * P
PAD_NODES = TILES * P

GROUP = 16
GROUPS = 7
CHUNKS = 3
CT = GROUP * GROUPS
SPAN = P // GROUP
KEYS = TILES * SPAN
assert CT * CHUNKS * P >= EDGES and CT <= P
FULL_TILES = EDGES // P
REST = EDGES - FULL_TILES * P
LAST_FULL = FULL_TILES - 2 * CT
STEP = GROUP * P * NODES // EDGES
SLACK = 28
CHUNK_STEP = STEP * GROUPS
WINDOW = (GROUPS - 1) * STEP + P
assert WINDOW <= 512
HCOLS = (CHUNKS - 1) * CHUNK_STEP + WINDOW

X_PARTS = [(0, 3), (3, 6), (6, TILES)]
NODE_TILES = [(0, 3), (3, 3), (6, 4)]
for _c, (_a, _n) in enumerate(NODE_TILES[:-1]):
    assert (_a + _n) * P <= (_c + 1) * CHUNK_STEP - SLACK


def schedule():
    ready, begun, order = [], [], []
    for g in range(CHUNKS * GROUPS + 1):
        if g and g % GROUPS == 0:
            a, n = NODE_TILES[g // GROUPS - 1]
            ready += list(range(a, a + n))
        order.append((g, advance(ready, begun)))
    while ready or begun:
        order.append((None, advance(ready, begun)))
    return order


NODE_STEPS = 4


def advance(ready, begun):
    nodes = [tuple(item) for item in begun]
    for item in list(begun):
        item[1] += 1
        if item[1] == NODE_STEPS:
            begun.remove(item)
    if ready:
        nodes.append((ready[0], 0))
        begun.append([ready.pop(0), 1])
    return nodes


SCHEDULE = schedule()

WS = 256.0
QUAD = 4
BATCH = 8
PAIRS = BATCH // 2

TOP = 2
SLOT_TILES = (TOP * NODES + EXPERTS * (P - 1)) // P
SLOTS = SLOT_TILES * P
BIG = float(1 << 20)

C_ID = 0
C_IOTA = C_ID + P
C_REP = C_IOTA + P
C_MASK = C_REP + P
C_START = C_MASK + GROUPS
C_DL = C_START + CHUNKS
C_LT = C_DL + 1
C_TRI = C_LT + EXPERTS * EXPERTS
C_VALID = C_TRI + P
C_M = C_VALID + TILES
C_TOKEN = C_M + SLOT_TILES * EXPERTS
NCONST = C_TOKEN + TILES


def constants():
    c = np.zeros((P, NCONST), np.float32)
    p = np.arange(P)
    c[:, C_ID:C_ID + P] = np.eye(P)
    c[:, C_IOTA:C_IOTA + P] = p[None, :]
    c[:CT, C_REP:C_REP + P] = (p[:CT, None] % GROUP) == (p[None, :] // SPAN)
    c[:CT, C_MASK:C_MASK + GROUPS] = (p[:CT, None] // GROUP) == np.arange(GROUPS)[None, :]
    c[:CT, C_START:C_START + CHUNKS] = (p[:CT, None] // GROUP) * STEP + np.arange(CHUNKS)[None, :] * CHUNK_STEP - SLACK
    c[:, C_DL] = p % SPAN
    i = np.arange(EXPERTS)
    c[:, C_LT:C_LT + 64] = (i[None, :] < i[:, None]).astype(np.float32).reshape(1, 64)
    c[:, C_TRI:C_TRI + P] = p[:, None] < p[None, :]
    c[:, C_VALID:C_VALID + TILES] = p[:, None] + P * np.arange(TILES)[None, :] < NODES
    node = p[:, None] + P * np.arange(TILES)[None, :]
    c[:, C_TOKEN:] = (node + 1) * (node < NODES)
    c[:, C_M:C_TOKEN] = np.repeat(np.arange(SLOT_TILES), EXPERTS)[None, :]
    return c


def gnn_moe_kernel(nc, x, src, dst, ew, w_gcn, b_gcn, w_fc, b_fc, w_r, w1, w2, const, out):
    ctx = ExitStack()
    with ctx:
        def sb(name, shape, dt=F32):
            return ctx.enter_context(nc.sbuf_tensor(name, shape, dt))

        def sem(name):
            return ctx.enter_context(nc.semaphore(name))

        cst = sb("cst", [P, NCONST])
        xs = sb("xs", [P, TILES, DIM])
        src_i = sb("src_i", [CT, CHUNKS, P], I32)
        dst_i = sb("dst_i", [CT, CHUNKS, P], I32)
        w_row = sb("w_row", [CT, CHUNKS, P])
        ROW_KEY, ROW_LO, ROW_W = range(3)
        rows = sb("rows", [CT, 3, CHUNKS, P])
        w_slow = sb("w_slow", [CT, CHUNKS, P])
        start_rel = sb("start_rel", [CT, CHUNKS])
        start_sel = sb("start_sel", [CT, CHUNKS, GROUPS])
        bad = sb("bad", [P, 1])
        bad_row = sb("bad_row", [1, 2])
        flag = sb("flag", [1, 1], I32)
        B_KEY, B_LO, B_W = 0, 1, 2
        edge_b = sb("edge_b", [P, 5, CHUNKS * CT], BF16)
        w_rem = sb("w_rem", [P, 2, CT])
        dval = sb("dval", [P, CHUNKS * GROUPS])
        iota_b = sb("iota_b", [P, P, 2], BF16)
        one_src = sb("one_src", [P, 2, PAIRS, P, 2], BF16)
        one_key = sb("one_key", [P, PAIRS, KEYS, 2], BF16)
        key_w = sb("key_w", [P, 2, 3, PAIRS, KEYS, 2], BF16)
        adj = sb("adj", [P, 2, TILES, GROUP * SPAN])
        part_h = sb("part_h", [P, HID])
        one_dst = sb("one_dst", [P, 2, P])
        hT = sb("hT", [P, HCOLS])
        wg = sb("wg", [P, KD, HID])
        wfc = sb("wfc", [P, KD, HID])
        wfcT = sb("wfcT", [P, DIM])
        bg = sb("bg", [P, 1])
        bfc = sb("bfc", [1, DIM])
        wr = sb("wr", [P, KD, EXPERTS])
        xg = sb("xg", [P, TILES, HID])
        stats = sb("stats", [P, TILES, 6])
        mv = sb("mv", [P, TILES, 2])
        std = sb("std", [P, TILES])
        rstd = sb("rstd", [P, TILES])
        nmr = sb("nmr", [P, TILES])
        xn = sb("xn", [P, TILES, DIM])
        xT = sb("xT", [P, 2, KD, P])
        ones = sb("ones", [1, P])
        stage = sb("stage", [P, 2, KD * FFN])
        w1_h = sb("w1_h", [P, EXPERTS, 2, KD, FFN], F16)
        w2_h = sb("w2_h", [P, EXPERTS, 2, KF, DIM], F16)
        lg = sb("lg", [P, TILES, EXPERTS])
        mx = sb("mx", [P, TILES])
        pr = sb("pr", [P, TILES, EXPERTS])
        sm = sb("sm", [P, TILES])
        cmp_gt = sb("cmp_gt", [P, TILES, EXPERTS, EXPERTS])
        cmp_eq = sb("cmp_eq", [P, TILES, EXPERTS, EXPERTS])
        rank = sb("rank", [P, TILES, EXPERTS])
        chosen = sb("chosen", [P, TILES, EXPERTS])
        chosen_b = sb("chosen_b", [P, TILES + 1, EXPERTS], BF16)
        tri_b = sb("tri_b", [P, P], BF16)
        ones_b = sb("ones_b", [P, P], BF16)
        n_i = sb("n_i", [P, EXPERTS], I32)
        tiles_i = sb("tiles_i", [P, EXPERTS], I32)
        tiles_f = sb("tiles_f", [P, EXPERTS])
        before = sb("before", [P, EXPERTS, EXPERTS])
        first = sb("first", [P, EXPERTS])
        first_slot = sb("first_slot", [P, EXPERTS])
        after = sb("after", [P, EXPERTS])
        slot = sb("slot", [P, TILES, EXPERTS])
        cand = sb("cand", [P, TOP, TILES, EXPERTS])
        slot_f = sb("slot_f", [P, TOP, TILES])
        slot_i = sb("slot_i", [P, TOP, TILES], I32)
        gate = sb("gate", [P, TOP, TILES])
        done_m = sb("done_m", [1, SLOT_TILES, EXPERTS])
        expert_f = sb("expert_f", [1, SLOT_TILES])
        expert_i = sb("expert_i", [1, SLOT_TILES], I32)
        place = sb("place", [P, 2, TOP, TILES], I32)
        place_b = sb("place_b", [P, 2, TOP, TILES], BF16)
        one_row = sb("one_row", [P, TOP, TILES // 2, P, 2], BF16)
        one_tile = sb("one_tile", [P, TOP, TILES, SLOT_TILES], BF16)
        node_at = sb("node_at", [P, TOP, TILES, SLOT_TILES], F16)
        tile_b = sb("tile_b", [P, SLOT_TILES], BF16)
        node_i = sb("node_i", [P, SLOT_TILES], I32)
        SB = 3
        xt_in = sb("xt_in", [P, SB, DIM])
        xT_h = sb("xT_h", [P, SB, 2, KD, P], F16)
        adj_flat = adj[:, :, :, :].rearrange("p a b s -> p (a b s)")
        hid = adj_flat[:, 0:SB * FFN].rearrange("p (s k n) -> p s k n", s=SB, k=KF)
        hid_h = adj_flat[:, SB * FFN:2 * SB * FFN].bitcast(F16).rearrange("p (s h k n) -> p s h k n", s=SB, h=2, k=KF)
        spare = xn[:, :, :].rearrange("p t d -> p (t d)")

        def edge_scratch(i, dt=F32):
            v = spare[0:CT, i * CHUNKS * P:(i + 1) * CHUNKS * P]
            return (v if dt == F32 else v.bitcast(dt)).rearrange("p (c e) -> p c e", c=CHUNKS)

        lo_i, hi_i = edge_scratch(0, I32), edge_scratch(1, I32)
        dl, rel, clip, ok_span, ok_win = (edge_scratch(i) for i in range(2, 7))
        YB = TILES // TOP
        y_in = xn[:, :, :].rearrange("p (b a) d -> p b a d", a=TOP)
        y_sb = stage[:, :, :].rearrange("p b (a d) -> p (b a) d", d=DIM)
        res = xt_in[:, 0:2, :]

        ident = cst[:, C_ID:C_ID + P]
        iota = cst[:, C_IOTA:C_IOTA + P]

        bank = [ctx.enter_context(nc.psum_tensor(f"bank{i}", [P, 512], F32)) for i in range(8)]
        ADJ = bank[0:2]
        AGG = bank[2]
        FC, TURN, LOGIT, POS, HT = bank[3], bank[4], bank[5], bank[6], bank[7]
        XT, HPRE, Y = bank[0:2], bank[2:4], bank[4:6]

        s_const, s_edges, s_w = sem("const_in"), sem("edges_in"), sem("w_in")
        s_x = [sem(f"x_in{i}") for i in range(3)]
        s_out = [sem("out_done0"), sem("out_done1")]
        s_pad = sem("pads_cleared")
        s_stage = [sem("stage_in0"), sem("stage_in1")]
        s_split = sem("expert_weights_split")
        s_scaled = sem("expert_weights_scaled")
        s_whi = sem("expert_weights_high")
        dv = sem("vector_step")
        ac = sem("scalar_step")
        s_rows = sem("edge_rows_ready")
        s_edgeT = sem("edge_rows_transposed")
        s_edgesc = sem("edge_scalars_ready")
        s_badT = sem("bad_transposed")
        s_flag = sem("flag_ready")
        s_dval = sem("window_rows_ready")
        s_mv = sem("norm_stats_ready")
        s_std = sem("norm_std_ready")
        s_rstd = sem("norm_scale_ready")
        s_xn = sem("normalised_ready")
        s_xnT = sem("normalised_transposed")
        s_xT = sem("transposed_copied")
        s_xT2 = sem("second_transposed_copied")
        s_xn2 = sem("second_normalised_ready")
        s_xg_ps = sem("xg_product")
        s_xg = sem("xg_ready")
        s_wfcT_ps = sem("wfc_transposed")
        s_wfcT = sem("wfc_ready")
        s_bfc_ps = sem("bfc_broadcast")
        s_xb = sem("x_plus_bias")
        s_okey = sem("key_one_hots_ready")
        s_one = sem("one_hots_ready")
        s_adj_ps = sem("adjacency_product")
        s_adj = sem("adjacency_copied")
        s_agg_ps = sem("aggregate_product")
        s_agg = sem("aggregate_copied")
        s_odst = sem("window_one_hot_ready")
        s_comb = sem("window_product")
        s_hT = sem("aggregate_added")
        s_fc = sem("fc_product")
        s_x2 = sem("x_plus_graph_layer")
        s_lg_ps = sem("logits_product")
        s_lg = sem("logits_copied")
        s_sub = sem("logits_less_max")
        s_exp = sem("exp_ready")
        s_chosen = sem("chosen_ready")
        s_pos = sem("positions_product")
        s_slot = sem("slots_ready")
        s_expert = sem("slot_tile_experts_ready")
        s_rowout = sem("normalised_rows_stored")
        s_ones = sem("slot_one_hots_ready")
        s_node_ps = sem("slot_nodes_product")
        s_node = sem("slot_nodes_ready")
        s_xin = [sem(f"slot_rows_in{i}") for i in range(3)]
        s_turn = sem("slot_rows_transposed")
        s_xh = sem("slot_high")
        s_xl = sem("slot_low")
        s_h = sem("hidden_product")
        s_gelu = sem("gelu_ready")
        s_hh = sem("hidden_high")
        s_hl = sem("hidden_low")
        s_y = sem("expert_product")
        s_ysb = sem("expert_output_copied")
        s_yout = [sem(f"expert_output_stored{i}") for i in range(3)]
        s_yin = [sem(f"expert_output_in{i}") for i in range(5)]
        s_acc = sem("first_expert_added")
        s_res = sem("result_ready")
        s_prep = sem("constants_cast")
        s_slowT = sem("slow_transposed")
        s_slow_sc = sem("slow_scalars")
        s_slow_v = sem("slow_operand_ready")
        s_slow_p = sem("slow_product_ready")
        s_slow_add = sem("slow_added")
        s_slow_iota = sem("slow_iota")

        cut = [0]

        def carve(rows_, n):
            cut[0] += n
            return spare[0:rows_, cut[0] - n:cut[0]]

        slow_turn = carve(P, PAD_NODES)
        slow_one = carve(P, PAD_NODES)
        slow_f = carve(CT, 2 * CHUNKS * P).rearrange("p (a c e) -> p a c e", a=2, c=CHUNKS)
        slow_sc = carve(P, 3 * CHUNKS * CT).rearrange("p (a t) -> p a t", a=3)
        slow_gw = carve(P, HID)
        slow_iota = adj[:, 0, :, :].rearrange("p b n -> p (b n)")
        x_rows = nc.dram_tensor("x_rows", [PAD_NODES, DIM], F32, kind="Internal").ap()
        y_slots = nc.dram_tensor("y_slots", [SLOTS, DIM], F32, kind="Internal").ap()
        block = ctx.enter_context(nc.Block())

        def edge_view(a, t0, n):
            return a[t0 * P:(t0 + n) * P].rearrange("(t e) -> t e", e=P)

        EDGE_DMAS = 3 * (CHUNKS + 1)
        W_DMAS = 5

        @block.sync
        def _(sp):
            def load_x(i, a, b):
                sp.dma_start(xs[:, a:b, :], x[a * P:b * P, :].rearrange("(t p) d -> p t d", p=P)).then_inc(s_x[i], 16)

            load_x(0, *X_PARTS[0])
            sp.wait_ge(s_pad, 1)
            for a, t in ((src, src_i), (dst, dst_i), (ew, w_row)):
                for c in range(CHUNKS):
                    n = CT if c < CHUNKS - 1 else LAST_FULL
                    sp.dma_start(t[0:n, c, :], edge_view(a, c * CT, n)).then_inc(s_edges, 16)
                sp.dma_start(t[LAST_FULL:LAST_FULL + 1, CHUNKS - 1, 0:REST],
                             a[FULL_TILES * P:EDGES].rearrange("(t e) -> t e", t=1)).then_inc(s_edges, 16)
            sp.dma_start(cst[:, :], const[:, :]).then_inc(s_const, 16)
            load_x(1, *X_PARTS[1])
            sp.wait_ge(s_pad, 2)
            load_x(2, X_PARTS[2][0], TILES - 1)
            sp.dma_start(xs[0:LAST_ROWS, TILES - 1, :], x[(TILES - 1) * P:NODES, :]).then_inc(s_x[2], 16)
            sp.dma_start(wg[:, :, :], w_gcn.rearrange("(k p) h -> p k h", p=P)).then_inc(s_w, 16)
            sp.dma_start(wfc[:, :, :], w_fc.rearrange("(k p) h -> p k h", p=P)).then_inc(s_w, 16)
            sp.dma_start(bg[:, :], b_gcn.rearrange("(p a) -> p a", a=1)).then_inc(s_w, 16)
            sp.dma_start(bfc[:, :], b_fc.rearrange("(a n) -> a n", a=1)).then_inc(s_w, 16)
            sp.dma_start(wr[:, :, :], w_r.rearrange("(k p) e -> p k e", p=P)).then_inc(s_w, 16)
            for n in range(2 * EXPERTS):
                e = n // 2
                if n >= 2:
                    sp.wait_ge(s_split, n - 1)
                w = w1[e].rearrange("(k p) f -> p k f", p=P) if n % 2 == 0 else w2[e].rearrange("(k p) d -> p k d", p=P)
                sp.dma_start(stage[:, n % 2, :].rearrange("p (k f) -> p k f", k=KD if n % 2 == 0 else KF), w)\
                  .then_inc(s_stage[n % 2], 16)

            for t in range(TILES):
                sp.wait_ge(s_xn2, t + 1)
                sp.dma_start(x_rows[t * P:(t + 1) * P, :], xn[:, t, :]).then_inc(s_rowout, 16)
            for m in range(SLOT_TILES):
                sp.wait_ge(s_ysb, m + 1)
                sp.dma_start(y_slots[m * P:(m + 1) * P, :], y_sb[:, m % SB, :]).then_inc(s_yout[m % SB], 16)
            for t in range(TILES):
                sp.wait_ge(s_res, t + 1)
                r = P if t < TILES - 1 else LAST_ROWS
                sp.dma_start(out[t * P:t * P + r, :], res[0:r, t % 2, :]).then_inc(s_out[t % 2], 16)
            for i in range(2):
                sp.wait_ge(s_out[i], 16 * (TILES // 2))

        @block.gpsimd
        def _(pool):
            for t in (src_i, dst_i):
                pool.memset(t[96:CT, CHUNKS - 1, :], 0)
            pool.memset(w_row[96:CT, CHUNKS - 1, :], 0.0).then_inc(s_pad, 1)
            pool.memset(xs[96:P, TILES - 1, :], 0.0).then_inc(s_pad, 1)
            for n in range(2 * EXPERTS):
                pool.wait_ge(s_whi, n + 1)
                dest = (w1_h if n % 2 == 0 else w2_h)[:, n // 2, :, :, :].rearrange("p s k f -> p s (k f)")
                pool.tensor_tensor(dest[:, 1, :], stage[:, n % 2, :], dest[:, 0, :], ALU.subtract).then_inc(s_split, 1)
            pool.wait_ge(s_rowout, 16 * TILES)
            pool.wait_ge(s_node, 1)
            for m in range(SLOT_TILES):
                if m >= SB:
                    pool.wait_ge(s_turn, m - SB + 1)
                pool.indirect_dma_start(out=xt_in[:, m % SB, :], out_offset=None, in_=x_rows[:, :],
                                        in_offset=bass.IndirectOffsetOnAxis(ap=node_i[:, m:m + 1], axis=0))\
                    .then_inc(s_xin[m % SB], 16)
            for i in range(SB):
                pool.wait_ge(s_yout[i], 16 * len(range(i, SLOT_TILES, SB)))
            for t in range(TILES):
                r = P if t < TILES - 1 else LAST_ROWS
                if t >= YB:
                    pool.wait_ge(s_res, t - YB + 1)
                for a in range(TOP):
                    pool.indirect_dma_start(out=y_in[0:r, t % YB, a, :], out_offset=None, in_=y_slots[:, :],
                                            in_offset=bass.IndirectOffsetOnAxis(ap=slot_i[0:r, a, t:t + 1], axis=0))\
                        .then_inc(s_yin[t % YB], 16)

        @block.scalar
        def _(act):
            def split_high(n):
                act.wait_ge(s_stage[n % 2], 16 * (n // 2 + 1))
                act.activation(stage[:, n % 2, :], stage[:, n % 2, :], ACT.Copy, scale=WS).then_inc(s_scaled, 1)
                act.wait_ge(s_scaled, n + 1)
                dest = (w1_h if n % 2 == 0 else w2_h)[:, n // 2, :, :, :].rearrange("p s k f -> p s (k f)")
                act.activation(dest[:, 0, :], stage[:, n % 2, :], ACT.Copy).then_inc(s_whi, 1)

            def copy_xg(t):
                act.wait_ge(s_xg_ps, t + 1)
                act.activation(xg[:, t, :], bank[2 + t % 2][:, 0:HID], ACT.Copy).then_inc(s_xg, 1)

            for i, (a, b) in enumerate(X_PARTS):
                act.wait_ge(s_mv, i + 1)
                act.activation(std[:, a:b], mv[:, a:b, 1], ACT.Sqrt).then_inc(s_std, 1)
                act.wait_ge(s_rstd, i + 1)
                for t in range(a, b):
                    act.activation(xn[:, t, :], xs[:, t, :], ACT.Identity, bias=nmr[:, t:t + 1],
                                   scale=rstd[:, t:t + 1]).then_inc(s_xn, 1)
                    if t >= 3:
                        copy_xg(t - 3)
            for t in range(TILES - 3, TILES):
                copy_xg(t)

            def edge_group(g):
                for i in range(GROUP // QUAD):
                    if i == GROUP // QUAD // 2 and g:
                        copy_agg(g - 1)
                    act.wait_ge(s_adj_ps, g * (GROUP // QUAD) + i + 1)
                    o = adj[:, g % 2, :, QUAD * i * SPAN:QUAD * (i + 1) * SPAN].rearrange("p b (t s) -> p t b s", t=QUAD)
                    act.activation(o, ADJ[i % 2][:, 0:QUAD * KEYS].rearrange("p (t b s) -> p t b s", t=QUAD, s=SPAN),
                                   ACT.Copy).then_inc(s_adj, 1)

            def copy_agg(g):
                act.wait_ge(s_agg_ps, g + 1)
                act.activation(part_h[:, :], AGG[:, 0:HID], ACT.Copy).then_inc(s_agg, 1)

            def node_step(t, k):
                if k == 0:
                    act.wait_ge(s_mv, 3 + t + 1)
                    act.activation(std[:, t:t + 1], mv[:, t, 1:2], ACT.Sqrt).then_inc(s_std, 1)
                if k == 1:
                    act.wait_ge(s_rstd, 3 + t + 1)
                    act.activation(xn[:, t, :], xs[:, t, :], ACT.Identity, bias=nmr[:, t:t + 1],
                                   scale=rstd[:, t:t + 1]).then_inc(s_xn2, 1)
                if k == 2:
                    act.wait_ge(s_xnT, TILES + t + 1)
                    if t >= 2:
                        act.wait_ge(s_lg_ps, t - 1)
                    act.activation(xT[:, t % 2, :, :], TURN[:, :].rearrange("p (k n) -> p k n", k=KD), ACT.Copy)\
                       .then_inc(s_xT2, 1)

            for g, nodes in SCHEDULE:
                if g is not None and g < CHUNKS * GROUPS:
                    edge_group(g)
                    if g < 2 * EXPERTS:
                        split_high(g)
                elif g is not None:
                    copy_agg(g - 1)
                for t, k in nodes:
                    node_step(t, k)
            act.wait_ge(s_sub, 1)
            act.activation(pr[:, :, :], lg[:, :, :], ACT.Exp).then_inc(s_exp, 1)

            def turned_high(m):
                act.wait_ge(s_turn, m + 1)
                if m >= SB:
                    act.wait_ge(s_h, m - SB + 1)
                act.activation(xT_h[:, m % SB, 0, :, :], XT[m % 2][:, :].rearrange("p (k n) -> p k n", k=KD),
                               ACT.Copy).then_inc(s_xh, 1)

            def gelu(m):
                act.wait_ge(s_h, m + 1)
                if m >= SB:
                    act.wait_ge(s_hl, m - SB + 1)
                    act.wait_ge(s_hh, m - SB + 1)
                act.activation(hid[:, m % SB, :, :], HPRE[m % 2][:, 0:KF * P].rearrange("p (k n) -> p k n", k=KF),
                               ACT.Gelu, scale=1.0 / WS).then_inc(s_gelu, 1)

            def copy_y(m):
                act.wait_ge(s_y, m + 1)
                if m >= SB:
                    act.wait_ge(s_yout[m % SB], 16 * (m // SB))
                act.activation(y_sb[:, m % SB, :], Y[m % 2][:, :], ACT.Copy, scale=1.0 / WS).then_inc(s_ysb, 1)

            for i in range(SLOT_TILES + 2):
                if i < SLOT_TILES:
                    turned_high(i)
                if 1 <= i <= SLOT_TILES:
                    gelu(i - 1)
                if i >= 2:
                    copy_y(i - 2)

        @block.vector
        def _(dve):
            steps = [0]

            def step(ins):
                steps[0] += 1
                ins.then_inc(dv, 1)
                dve.wait_ge(dv, steps[0])

            def norm_stats(a, b):
                for t in range(a, b):
                    ins = dve.bn_stats(stats[:, t, :], xs[:, t, :])
                step(ins)
                for t in range(a, b):
                    ins = dve.bn_aggr(mv[:, t, :], stats[:, t, :])
                step(ins)
                dve.tensor_scalar(mv[:, a:b, 1], mv[:, a:b, 1], EPS, None, ALU.add).then_inc(s_mv, 1)

            def norm_scale(a, b, count):
                dve.wait_ge(s_std, count + 1)
                step(dve.reciprocal(rstd[:, a:b], std[:, a:b]))
                dve.scalar_tensor_tensor(out=nmr[:, a:b], in0=mv[:, a:b, 0], scalar=-1.0,
                                         in1=rstd[:, a:b], op0=ALU.mult, op1=ALU.mult).then_inc(s_rstd, 1)

            def norm_x(i):
                dve.wait_ge(s_x[i], 16 if i < 2 else 32)
                norm_stats(*X_PARTS[i])
                norm_scale(*X_PARTS[i], i)

            def copy_xT(t):
                dve.wait_ge(s_xnT, t + 1)
                if t >= 2:
                    dve.wait_ge(s_xg_ps, t - 1)
                dve.tensor_copy(xT[:, t % 2, :, :], bank[t % 2][:, :].rearrange("p (k n) -> p k n", k=KD))\
                   .then_inc(s_xT, 1)

            dve.wait_ge(s_edges, 16 * EDGE_DMAS)
            dve.wait_ge(s_const, 16)
            dve.wait_ge(s_pad, 1)
            dve.tensor_scalar(lo_i[:, :, :], src_i[:, :, :], P - 1, None, ALU.bitwise_and)
            dve.tensor_scalar(hi_i[:, :, :], src_i[:, :, :], 7, None, ALU.logical_shift_right)
            dve.tensor_tensor(dl[:, :, :], dst_i[:, :, :], dst_i[:, :, 0:1].broadcast_to([CT, CHUNKS, P]), ALU.subtract)
            starts = cst[0:CT, C_START:C_START + CHUNKS]
            dve.tensor_tensor(rel[:, :, :], dst_i[:, :, :],
                              starts.rearrange("p (c o) -> p c o", o=1).broadcast_to([CT, CHUNKS, P]), ALU.subtract)
            step(dve.tensor_tensor(start_rel[:, :], dst_i[:, :, 0], starts, ALU.subtract))
            dve.tensor_copy(rows[:, ROW_LO, :, :], lo_i[:, :, :])
            dve.scalar_tensor_tensor(out=rows[:, ROW_KEY, :, :], in0=hi_i[:, :, :], scalar=float(SPAN),
                                     in1=dl[:, :, :], op0=ALU.mult, op1=ALU.add)
            step(dve.tensor_scalar(clip[:, :, :], dl[:, :, :], 0.0, float(SPAN - 1), ALU.max, ALU.min))
            step(dve.tensor_tensor(ok_span[:, :, :], clip[:, :, :], dl[:, :, :], ALU.is_equal))
            step(dve.tensor_scalar(clip[:, :, :], rel[:, :, :], 0.0, float(P - 1), ALU.max, ALU.min))
            step(dve.tensor_tensor(ok_win[:, :, :], clip[:, :, :], rel[:, :, :], ALU.is_equal))
            step(dve.tensor_tensor(ok_span[:, :, :], ok_span[:, :, :], ok_win[:, :, :], ALU.mult))
            step(dve.tensor_tensor(rows[:, ROW_W, :, :], w_row[:, :, :], ok_span[:, :, :], ALU.mult))
            dve.tensor_tensor(start_sel[:, :, :],
                              start_rel[:, :].rearrange("p (c o) -> p c o", o=1).broadcast_to([CT, CHUNKS, GROUPS]),
                              cst[0:CT, C_MASK:C_MASK + GROUPS].rearrange("p (o j) -> p o j", o=1)
                              .broadcast_to([CT, CHUNKS, GROUPS]), ALU.mult)
            dve.memset(bad[:, :], 0.0)
            step(dve.tensor_tensor(w_slow[:, :, :], w_row[:, :, :], rows[:, ROW_W, :, :], ALU.subtract))
            dve.tensor_reduce(bad[0:CT, :], w_slow[:, :, :], AX.XY, ALU.max, apply_absolute_value=True)\
               .then_inc(s_rows, 1)
            dve.tensor_copy(iota_b[:, :, :], iota.rearrange("p (n o) -> p n o", o=1).broadcast_to([P, P, 2]))
            dve.tensor_copy(tile_b[:, :], iota[:, 0:SLOT_TILES])
            dve.tensor_copy(tri_b[:, :], cst[:, C_TRI:C_TRI + P])
            dve.memset(ones_b[:, :], 1.0)
            dve.memset(ones[:, :], 1.0)
            dve.memset(chosen_b[:, :, :], 0.0)
            dve.wait_ge(s_w, 16 * W_DMAS)
            step(dve.memset(hT[:, :], 0.0))
            dve.tensor_scalar(hT[:, :], hT[:, :], bg[:, 0:1], None, ALU.add).then_inc(s_prep, 1)
            dve.wait_ge(s_badT, 1)
            step(dve.tensor_reduce(bad_row[:, 0:1], bank[6][0:1, 0:P], AX.X, ALU.max))
            step(dve.tensor_scalar(bad_row[:, 1:2], bad_row[:, 0:1], 0.0, None, ALU.is_gt))
            dve.tensor_copy(flag[:, :], bad_row[:, 1:2]).then_inc(s_flag, 1)
            dve.wait_ge(s_edgeT, CHUNKS + 1)
            dve.tensor_scalar(dval[:, :], bank[7][:, 0:CHUNKS * GROUPS], cst[:, C_DL:C_DL + 1], None, ALU.add)\
               .then_inc(s_dval, 1)
            for c in range(CHUNKS):
                col = slice(c * CT, (c + 1) * CT)
                w = bank[3 + c][:, 2 * CT:3 * CT]
                dve.tensor_copy(edge_b[:, 0:2, col], bank[3 + c][:, 0:2 * CT].rearrange("p (a t) -> p a t", a=2))
                step(dve.tensor_copy(edge_b[:, B_W, col], w))
                step(dve.tensor_tensor(w_rem[:, 0, :], w, edge_b[:, B_W, col], ALU.subtract))
                step(dve.tensor_copy(edge_b[:, B_W + 1, col], w_rem[:, 0, :]))
                dve.tensor_tensor(edge_b[:, B_W + 2, col], w_rem[:, 0, :], edge_b[:, B_W + 1, col],
                                  ALU.subtract).then_inc(s_edgesc, 1)
                dve.wait_ge(s_edgesc, c + 1)

            norm_x(0)
            norm_x(1)
            for t in range(3):
                copy_xT(t)
            norm_x(2)
            for t in range(3, TILES):
                copy_xT(t)
            dve.wait_ge(s_bfc_ps, 1)
            dve.wait_ge(s_xn, TILES)
            for t in range(TILES):
                dve.tensor_tensor(xs[:, t, :], xs[:, t, :], bank[7][:, :], ALU.add).then_inc(s_xb, 1)
            dve.wait_ge(s_wfcT_ps, 1)
            dve.tensor_copy(wfcT[:, :], bank[6][:, :]).then_inc(s_wfcT, 1)

            slow = dve.value_load(flag[0:1, 0:1], min_val=0, max_val=1)
            with dve.If(slow > 0):
                dve.tensor_copy(slow_f[:, 0, :, :], src_i[:, :, :])
                dve.tensor_copy(slow_f[:, 1, :, :], dst_i[:, :, :]).then_inc(s_slow_sc, 1)
                dve.wait_ge(s_slowT, 1)
                for c in range(CHUNKS):
                    dve.tensor_copy(slow_sc[:, :, c * CT:(c + 1) * CT],
                                    bank[c][:, 0:3 * CT].rearrange("p (a t) -> p a t", a=3)).then_inc(s_slow_sc, 1)
                dve.wait_ge(s_slow_sc, 1 + CHUNKS)
                for b in range(TILES):
                    ins = dve.tensor_scalar(slow_iota[:, b * P:(b + 1) * P], iota, float(b * P), None, ALU.add)
                ins.then_inc(s_slow_iota, 1)
                dve.wait_ge(s_slow_iota, 1)
                with dve.Fori(0, FULL_TILES + 1) as t:
                    dve.tensor_scalar(slow_one[:, :], slow_iota, slow_sc[:, 0, bass.ds(t, 1)], None,
                                      ALU.is_equal).then_inc(s_slow_v, 1)
                    dve.wait_ge(s_slow_p, t * 3 + 1)
                    for b in range(3):
                        w = min(512, PAD_NODES - 512 * b)
                        dve.tensor_copy(slow_turn[:, 512 * b:512 * b + w], bank[3 + b][:, 0:w])
                    dve.tensor_scalar(slow_one[:, :], slow_iota, slow_sc[:, 1, bass.ds(t, 1)], None,
                                      ALU.is_equal).then_inc(s_slow_v, 1)
                    dve.wait_ge(s_slow_p, t * 3 + 2)
                    dve.tensor_scalar(slow_gw[:, :], bank[2][:, 0:HID], slow_sc[:, 2, bass.ds(t, 1)], None,
                                      ALU.mult).then_inc(s_slow_v, 1)
                    dve.wait_ge(s_slow_p, t * 3 + 3)
                    for b in range(3):
                        w = min(512, PAD_NODES - 512 * b)
                        ins = dve.tensor_tensor(hT[:, SLACK + 512 * b:SLACK + 512 * b + w], bank[3 + b][:, 0:w],
                                                hT[:, SLACK + 512 * b:SLACK + 512 * b + w], ALU.add)
                    ins.then_inc(s_slow_add, 1)
                    dve.wait_ge(s_slow_add, t + 1)
            dve.end_ifs()

            def edge_group(g):
                for i in range(GROUP // BATCH):
                    b = g * (GROUP // BATCH) + i
                    r = b % 2
                    if b >= 2:
                        dve.wait_ge(s_adj_ps, (b - 1) * (BATCH // QUAD))
                    t0 = b * BATCH

                    def edges(a):
                        return edge_b[:, a, t0:t0 + BATCH].rearrange("p (q o u) -> p q o u", o=1, u=2)

                    def labels(n):
                        return iota_b[:, 0:n, :].rearrange("p (o n) u -> p o n u", o=1).broadcast_to([P, PAIRS, n, 2])

                    if b:
                        dve.wait_ge(s_one, b)
                    dve.tensor_tensor(one_key[:, :, :, :], labels(KEYS),
                                      edges(B_KEY).broadcast_to([P, PAIRS, KEYS, 2]), ALU.is_equal).then_inc(s_okey, 1)
                    dve.tensor_tensor(one_src[:, r, :, :, :], labels(P),
                                      edges(B_LO).broadcast_to([P, PAIRS, P, 2]), ALU.is_equal)
                    dve.wait_ge(s_okey, b + 1)
                    for k in range(3):
                        ins = dve.tensor_tensor(key_w[:, r, k, :, :, :], one_key[:, :, :, :],
                                                edges(B_W + k).broadcast_to([P, PAIRS, KEYS, 2]), ALU.mult)
                    ins.then_inc(s_one, 1)
                if g >= 2:
                    dve.wait_ge(s_comb, g - 1)
                dve.tensor_scalar(one_dst[:, g % 2, :], iota, dval[:, g:g + 1], None, ALU.is_equal).then_inc(s_odst, 1)

            def add_chunk(c):
                dve.wait_ge(s_comb, (c + 1) * GROUPS)
                cols = slice(c * CHUNK_STEP, c * CHUNK_STEP + WINDOW)
                dve.tensor_tensor(hT[:, cols], HT[:, 0:WINDOW], hT[:, cols], ALU.add).then_inc(s_hT, 1)
                dve.wait_ge(s_hT, c + 1)

            def node_step(t, k):
                if k == 0:
                    dve.wait_ge(s_fc, t + 1)
                    step(dve.tensor_tensor(xs[:, t, :], FC[:, :], xs[:, t, :], ALU.add))
                    norm_stats(t, t + 1)
                if k == 1:
                    norm_scale(t, t + 1, 3 + t)
                if k == 3:
                    dve.wait_ge(s_lg_ps, t + 1)
                    dve.tensor_copy(lg[:, t, :], LOGIT[:, 0:EXPERTS]).then_inc(s_lg, 1)

            for g, nodes in SCHEDULE:
                if g is not None:
                    if g < CHUNKS * GROUPS:
                        edge_group(g)
                    if g and g % GROUPS == 0:
                        add_chunk(g // GROUPS - 1)
                for t, k in nodes:
                    node_step(t, k)

            def along(t2, inner):
                return t2.rearrange("p (n o) -> p n o", o=1).broadcast_to([P, TILES, inner])

            dve.wait_ge(s_lg, TILES)
            step(dve.tensor_reduce(mx[:, :], lg[:, :, :], AX.X, ALU.max))
            dve.tensor_tensor(lg[:, :, :], lg[:, :, :], along(mx[:, :], EXPERTS), ALU.subtract).then_inc(s_sub, 1)
            dve.wait_ge(s_exp, 1)
            step(dve.tensor_reduce(sm[:, :], pr[:, :, :], AX.X, ALU.add))
            step(dve.reciprocal(sm[:, :], sm[:, :]))
            step(dve.tensor_tensor(pr[:, :, :], pr[:, :, :], along(sm[:, :], EXPERTS), ALU.mult))
            square = [P, TILES, EXPERTS, EXPERTS]
            pj = pr[:, :, :].rearrange("p n (o j) -> p n o j", o=1).broadcast_to(square)
            pi = pr[:, :, :].rearrange("p n (i o) -> p n i o", o=1).broadcast_to(square)
            lt = cst[:, C_LT:C_LT + EXPERTS * EXPERTS].rearrange("p (o i j) -> p o i j", o=1, i=EXPERTS)
            dve.tensor_tensor(cmp_gt[:, :, :, :], pj, pi, ALU.is_gt)
            step(dve.tensor_tensor(cmp_eq[:, :, :, :], pj, pi, ALU.is_equal))
            step(dve.tensor_tensor(cmp_eq[:, :, :, :], cmp_eq[:, :, :, :], lt.broadcast_to(square), ALU.mult))
            step(dve.tensor_tensor(cmp_gt[:, :, :, :], cmp_gt[:, :, :, :], cmp_eq[:, :, :, :], ALU.add))
            step(dve.tensor_reduce(rank[:, :, :], cmp_gt[:, :, :, :], AX.X, ALU.add))
            step(dve.tensor_scalar(rank[:, :, :], rank[:, :, :], TOP - 0.5, None, ALU.is_lt))
            step(dve.tensor_tensor(chosen[:, :, :], rank[:, :, :],
                                   along(cst[:, C_VALID:C_VALID + TILES], EXPERTS), ALU.mult))
            dve.tensor_copy(chosen_b[:, 0:TILES, :], chosen[:, :, :]).then_inc(s_chosen, 1)
            dve.tensor_tensor(pr[:, :, :], pr[:, :, :], chosen[:, :, :], ALU.mult)
            dve.wait_ge(s_pos, 1)
            step(dve.tensor_scalar(n_i[:, :], POS[:, TILES * EXPERTS:(TILES + 1) * EXPERTS], float(P - 1), None, ALU.add))
            step(dve.tensor_scalar(tiles_i[:, :], n_i[:, :], 7, None, ALU.logical_shift_right))
            step(dve.tensor_copy(tiles_f[:, :], tiles_i[:, :]))
            step(dve.tensor_tensor(before[:, :, :],
                                   tiles_f[:, :].rearrange("p (o j) -> p o j", o=1).broadcast_to([P, EXPERTS, EXPERTS]),
                                   cst[:, C_LT:C_LT + EXPERTS * EXPERTS].rearrange("p (i j) -> p i j", i=EXPERTS), ALU.mult))
            step(dve.tensor_reduce(first[:, :], before[:, :, :], AX.X, ALU.add))
            dve.tensor_tensor(after[:, :], first[:, :], tiles_f[:, :], ALU.add)
            step(dve.tensor_scalar(first_slot[:, :], first[:, :], float(P), None, ALU.mult))
            step(dve.tensor_tensor(slot[:, :, :], POS[:, 0:TILES * EXPERTS].rearrange("p (t e) -> p t e", t=TILES),
                                   first_slot[:, :].rearrange("p (o e) -> p o e", o=1)
                                   .broadcast_to([P, TILES, EXPERTS]), ALU.add))
            step(dve.tensor_tensor(cand[:, 1, :, :], slot[:, :, :], chosen[:, :, :], ALU.mult))
            step(dve.tensor_scalar(rank[:, :, :], chosen[:, :, :], -BIG, BIG, ALU.mult, ALU.add))
            step(dve.tensor_tensor(cand[:, 0, :, :], cand[:, 1, :, :], rank[:, :, :], ALU.add))
            dve.tensor_reduce(slot_f[:, 0, :], cand[:, 0, :, :], AX.X, ALU.min)
            step(dve.tensor_reduce(slot_f[:, 1, :], cand[:, 1, :, :], AX.X, ALU.max))
            step(dve.tensor_copy(slot_i[:, :, :], slot_f[:, :, :]))
            dve.tensor_scalar(place[:, 0, :, :], slot_i[:, :, :], P - 1, None, ALU.bitwise_and)
            step(dve.tensor_scalar(place[:, 1, :, :], slot_i[:, :, :], 7, None, ALU.logical_shift_right))
            step(dve.tensor_copy(place_b[:, :, :, :], place[:, :, :, :]))
            for a in range(TOP):
                dve.tensor_tensor(one_row[:, a, :, :, :],
                                  iota_b[:, :, :].rearrange("p (o n) u -> p o n u", o=1).broadcast_to([P, TILES // 2, P, 2]),
                                  place_b[:, 0, a, :].rearrange("p (q o u) -> p q o u", o=1, u=2)
                                  .broadcast_to([P, TILES // 2, P, 2]), ALU.is_equal)
            wide = [P, TOP, TILES, SLOT_TILES]
            for a in range(TOP):
                ins = dve.tensor_tensor(one_tile[:, a, :, :],
                                        tile_b[:, :].rearrange("p (o m) -> p o m", o=1).broadcast_to(wide[:1] + wide[2:]),
                                        place_b[:, 1, a, :].rearrange("p (t o) -> p t o", o=1)
                                        .broadcast_to(wide[:1] + wide[2:]), ALU.is_equal)
            step(ins)
            for a in range(TOP):
                ins = dve.tensor_tensor(node_at[:, a, :, :], one_tile[:, a, :, :],
                                        cst[:, C_TOKEN:C_TOKEN + TILES].rearrange("p (t o) -> p t o", o=1)
                                        .broadcast_to(wide[:1] + wide[2:]), ALU.mult)
            ins.then_inc(s_ones, 1)
            dve.wait_ge(s_node_ps, 1)
            dve.tensor_scalar(node_i[:, :], POS[:, 0:SLOT_TILES], -1.0, 0.0, ALU.add, ALU.max).then_inc(s_node, 1)
            step(dve.tensor_tensor(done_m[:, :, :], cst[0:1, C_M:C_M + SLOT_TILES * EXPERTS]
                                   .rearrange("p (m e) -> p m e", e=EXPERTS),
                                   after[0:1, :].rearrange("p (o e) -> p o e", o=1)
                                   .broadcast_to([1, SLOT_TILES, EXPERTS]), ALU.is_ge))
            step(dve.tensor_reduce(expert_f[:, :], done_m[:, :, :], AX.X, ALU.add))
            dve.tensor_scalar(expert_i[:, :], expert_f[:, :], float(EXPERTS - 1), None, ALU.min).then_inc(s_expert, 1)
            for a in range(TOP):
                step(dve.tensor_tensor(cand[:, a, :, :], cand[:, a, :, :], along(slot_f[:, a, :], EXPERTS), ALU.is_equal))
                step(dve.tensor_tensor(cand[:, a, :, :], cand[:, a, :, :], pr[:, :, :], ALU.mult))
                step(dve.tensor_reduce(gate[:, a, :], cand[:, a, :, :], AX.X, ALU.add))

            def turned_low(m):
                dve.wait_ge(s_xh, m + 1)
                if m >= SB:
                    dve.wait_ge(s_h, m - SB + 1)
                dve.tensor_tensor(xT_h[:, m % SB, 1, :, :], XT[m % 2][:, :].rearrange("p (k n) -> p k n", k=KD),
                                  xT_h[:, m % SB, 0, :, :], ALU.subtract).then_inc(s_xl, 1)

            def hidden_halves(m):
                dve.wait_ge(s_gelu, m + 1)
                if m >= SB:
                    dve.wait_ge(s_y, m - SB + 1)
                dve.tensor_copy(hid_h[:, m % SB, 0, :, :], hid[:, m % SB, :, :]).then_inc(s_hh, 1)
                dve.wait_ge(s_hh, m + 1)
                dve.tensor_tensor(hid_h[:, m % SB, 1, :, :], hid[:, m % SB, :, :], hid_h[:, m % SB, 0, :, :],
                                  ALU.subtract).then_inc(s_hl, 1)

            for i in range(SLOT_TILES + 1):
                if i < SLOT_TILES:
                    turned_low(i)
                if i >= 1:
                    hidden_halves(i - 1)

            for t in range(TILES):
                r = P if t < TILES - 1 else LAST_ROWS
                dve.wait_ge(s_yin[t % YB], 32 * (t // YB + 1))
                dve.scalar_tensor_tensor(out=xs[0:r, t, :], in0=y_in[0:r, t % YB, 0, :], scalar=gate[0:r, 0, t:t + 1],
                                         in1=xs[0:r, t, :], op0=ALU.mult, op1=ALU.add).then_inc(s_acc, 1)
                dve.wait_ge(s_acc, t + 1)
                if t >= 2:
                    dve.wait_ge(s_out[t % 2], 16 * (t // 2))
                dve.scalar_tensor_tensor(out=res[0:r, t % 2, :], in0=y_in[0:r, t % YB, 1, :],
                                         scalar=gate[0:r, 1, t:t + 1], in1=xs[0:r, t, :],
                                         op0=ALU.mult, op1=ALU.add).then_inc(s_res, 1)

        @block.tensor
        def _(pe):
            pe.wait_ge(s_const, 16)
            pe.wait_ge(s_rows, 1)
            pe.transpose(bank[6][0:1, 0:P], bad[:, 0:1], ident).then_inc(s_badT, 1)
            for c in range(CHUNKS):
                for a in range(3):
                    ins = pe.transpose(bank[3 + c][:, a * CT:(a + 1) * CT], rows[:, a, c, :], cst[0:CT, C_ID:C_ID + CT])
                ins.then_inc(s_edgeT, 1)
            pe.matmul(bank[7][:, 0:CHUNKS * GROUPS], cst[0:CT, C_REP:C_REP + P],
                      start_sel[:, :, :].rearrange("p c j -> p (c j)"), start=True, stop=True).then_inc(s_edgeT, 1)
            pe.wait_ge(s_w, 16 * W_DMAS)

            def turn_x(t):
                pe.wait_ge(s_xn, t + 1)
                if t >= 2:
                    pe.wait_ge(s_xT, t - 1)
                for k in range(KD):
                    ins = pe.transpose(bank[t % 2][:, k * P:(k + 1) * P], xn[:, t, k * P:(k + 1) * P], ident)
                ins.then_inc(s_xnT, 1)

            def product_x(t):
                pe.wait_ge(s_xT, t + 1)
                if t >= 2:
                    pe.wait_ge(s_xg, t - 1)
                if t == 1:
                    pe.wait_ge(s_edgesc, 1)
                for k in range(KD):
                    ins = pe.matmul(bank[2 + t % 2][:, 0:HID], xT[:, t % 2, k, :], wg[:, k, :],
                                    start=(k == 0), stop=(k == KD - 1))
                ins.then_inc(s_xg_ps, 1)

            for t in range(TILES + 1):
                if t < TILES:
                    turn_x(t)
                if t:
                    product_x(t - 1)
            pe.wait_ge(s_dval, 1)
            pe.matmul(bank[7][:, :], ones[0:1, :], bfc[:, :],
                      start=True, stop=True).then_inc(s_bfc_ps, 1)
            pe.wait_ge(s_flag, 1)
            for k in range(KD):
                ins = pe.transpose(bank[6][:, k * P:(k + 1) * P], wfc[:, k, :], ident)
            ins.then_inc(s_wfcT_ps, 1)

            slow = pe.value_load(flag[0:1, 0:1], min_val=0, max_val=1)
            with pe.If(slow > 0):
                pe.wait_ge(s_slow_sc, 1)
                pe.wait_ge(s_xg, TILES)
                for c in range(CHUNKS):
                    for a in range(3):
                        row = slow_f[:, a, c, :] if a < 2 else w_slow[:, c, :]
                        ins = pe.transpose(bank[c][:, a * CT:(a + 1) * CT], row, cst[0:CT, C_ID:C_ID + CT])
                ins.then_inc(s_slowT, 1)
                pe.wait_ge(s_slow_sc, 1 + CHUNKS)
                with pe.Fori(0, FULL_TILES + 1) as t:
                    pe.wait_ge(s_slow_v, t * 3 + 1)
                    for b in range(TILES):
                        ins = pe.transpose(bank[3 + b // 4][:, (b % 4) * P:(b % 4 + 1) * P],
                                           slow_one[:, b * P:(b + 1) * P], ident)
                    ins.then_inc(s_slow_p, 1)
                    pe.wait_ge(s_slow_v, t * 3 + 2)
                    for b in range(TILES):
                        ins = pe.matmul(bank[2][:, 0:HID], slow_turn[:, b * P:(b + 1) * P], xg[:, b, :],
                                        start=(b == 0), stop=(b == TILES - 1))
                    ins.then_inc(s_slow_p, 1)
                    pe.wait_ge(s_slow_v, t * 3 + 3)
                    for b in range(3):
                        w = min(512, PAD_NODES - 512 * b)
                        ins = pe.matmul(bank[3 + b][:, 0:w], slow_gw[:, :], slow_one[:, 512 * b:512 * b + w],
                                        start=True, stop=True)
                    ins.then_inc(s_slow_p, 1)
                pe.wait_ge(s_slow_add, FULL_TILES + 1)
            pe.end_ifs()
            pe.wait_ge(s_xg, TILES)
            pe.wait_ge(s_wfcT, 1)
            pe.wait_ge(s_xb, TILES)
            pe.wait_ge(s_prep, 1)

            def edge_group(g):
                for i in range(GROUP):
                    t = g * GROUP + i
                    if i == BATCH and g:
                        aggregate(g - 1)
                    if i % BATCH == 0:
                        pe.wait_ge(s_one, t // BATCH + 1)
                    if i % QUAD == 0 and t >= 2 * QUAD:
                        pe.wait_ge(s_adj, t // QUAD - 1)
                    o = ADJ[i // QUAD % 2][:, i % QUAD * KEYS:(i % QUAD + 1) * KEYS]
                    r, q, u = t // BATCH % 2, i % BATCH // 2, i % 2
                    for k in range(3):
                        ins = pe.matmul(o, one_src[:, r, q, :, u], key_w[:, r, k, q, :, u],
                                        start=(k == 0), stop=(k == 2))
                    if i % QUAD == QUAD - 1:
                        ins.then_inc(s_adj_ps, 1)

            def aggregate(g):
                pe.wait_ge(s_adj, (g + 1) * (GROUP // QUAD))
                if g >= 1:
                    pe.wait_ge(s_agg, g)
                for b in range(TILES):
                    ins = pe.matmul(AGG[:, 0:HID], adj[:, g % 2, b, :], xg[:, b, :], start=(b == 0), stop=(b == TILES - 1))
                ins.then_inc(s_agg_ps, 1)

            def combine(g):
                j = g % GROUPS
                pe.wait_ge(s_agg, g + 1)
                pe.wait_ge(s_odst, g + 1)
                if j == 0 and g:
                    pe.wait_ge(s_hT, g // GROUPS)
                pe.matmul(HT[:, j * STEP:j * STEP + P], part_h[:, :], one_dst[:, g % 2, :], start=(j == 0),
                          stop=(j == GROUPS - 1), skip_group_check=True).then_inc(s_comb, 1)

            def node_step(t, k):
                if k == 0:
                    if t:
                        pe.wait_ge(s_mv, 3 + t)
                    pe.wait_ge(s_hT, next(c for c, (a, n) in enumerate(NODE_TILES) if t < a + n) + 1)
                    pe.matmul(FC[:, :], hT[:, SLACK + t * P:SLACK + (t + 1) * P], wfcT[:, :],
                              start=True, stop=True).then_inc(s_fc, 1)
                if k == 2:
                    pe.wait_ge(s_xn2, t + 1)
                    if t:
                        pe.wait_ge(s_xT2, t)
                    for k in range(KD):
                        ins = pe.transpose(TURN[:, k * P:(k + 1) * P], xn[:, t, k * P:(k + 1) * P], ident)
                    ins.then_inc(s_xnT, 1)
                elif k == 3:
                    pe.wait_ge(s_xT2, t + 1)
                    if t:
                        pe.wait_ge(s_lg, t)
                    for k in range(KD):
                        ins = pe.matmul(LOGIT[:, 0:EXPERTS], xT[:, t % 2, k, :], wr[:, k, :],
                                        start=(k == 0), stop=(k == KD - 1))
                    ins.then_inc(s_lg_ps, 1)

            for g, nodes in SCHEDULE:
                if g is not None:
                    if g < CHUNKS * GROUPS:
                        edge_group(g)
                    else:
                        aggregate(g - 1)
                    if g:
                        combine(g - 1)
                for t, k in nodes:
                    node_step(t, k)

            pe.wait_ge(s_chosen, 1)
            pe.matmul(POS[:, 0:(TILES + 1) * EXPERTS], tri_b[:, :], chosen_b[:, :, :].rearrange("p t e -> p (t e)"),
                      start=True, stop=False, skip_group_check=True)
            for t in range(TILES):
                n = TILES - t
                ins = pe.matmul(POS[:, (t + 1) * EXPERTS:(TILES + 1) * EXPERTS], ones_b[:, :],
                                chosen_b[:, t:t + 1, :].broadcast_to([P, n, EXPERTS]),
                                start=False, stop=(t == TILES - 1), skip_group_check=True)
            ins.then_inc(s_pos, 1)
            pe.wait_ge(s_ones, 1)
            for a in range(TOP):
                for t in range(TILES):
                    ins = pe.matmul(POS[:, 0:SLOT_TILES], one_row[:, a, t // 2, :, t % 2], node_at[:, a, t, :],
                                    start=(a == 0 and t == 0), stop=(a == TOP - 1 and t == TILES - 1))
            ins.then_inc(s_node_ps, 1)
            pe.wait_ge(s_split, 2 * EXPERTS)
            pe.wait_ge(s_lg, TILES)
            pe.wait_ge(s_expert, 1)

            def turn(m):
                pe.wait_ge(s_xin[m % SB], 16 * (m // SB + 1))
                if m >= 2:
                    pe.wait_ge(s_xl, m - 1)
                for k in range(KD):
                    ins = pe.transpose(XT[m % 2][:, k * P:(k + 1) * P], xt_in[:, m % SB, k * P:(k + 1) * P], ident)
                ins.then_inc(s_turn, 1)

            def up(m):
                e = pe.value_load(expert_i[0:1, m:m + 1], min_val=0, max_val=EXPERTS - 1)
                pe.wait_ge(s_xh, m + 1)
                pe.wait_ge(s_xl, m + 1)
                if m >= 2:
                    pe.wait_ge(s_gelu, m - 1)
                terms = [(w_h, x_h, k) for w_h, x_h in ((0, 0), (0, 1), (1, 0)) for k in range(KD)]
                for f in range(KF):
                    for i, (w_h, x_h, k) in enumerate(terms):
                        w = w1_h[:, bass.ds(e, 1), w_h, k, f * P:(f + 1) * P].rearrange("p o f -> p (o f)")
                        ins = pe.matmul(HPRE[m % 2][:, f * P:(f + 1) * P], w, xT_h[:, m % SB, x_h, k, :],
                                        start=(i == 0), stop=(i == len(terms) - 1))
                ins.then_inc(s_h, 1)
                return e

            def down(m, e):
                pe.wait_ge(s_hh, m + 1)
                pe.wait_ge(s_hl, m + 1)
                if m >= 2:
                    pe.wait_ge(s_ysb, m - 1)
                terms = [(h_h, w_h, k) for k in range(KF) for h_h, w_h in ((0, 0), (0, 1), (1, 0))]
                for i, (h_h, w_h, k) in enumerate(terms):
                    w = w2_h[:, bass.ds(e, 1), w_h, k, :].rearrange("p o d -> p (o d)")
                    ins = pe.matmul(Y[m % 2][:, :], hid_h[:, m % SB, h_h, k, :], w,
                                    start=(i == 0), stop=(i == len(terms) - 1))
                ins.then_inc(s_y, 1)

            experts = {}
            for i in range(SLOT_TILES + 2):
                if i < SLOT_TILES:
                    turn(i)
                if 1 <= i <= SLOT_TILES:
                    experts[i - 1] = up(i - 1)
                if i >= 2:
                    down(i - 2, experts.pop(i - 2))


_INS = ["x", "src", "dst", "edge_weight", "L0_gnn_W_gcn", "L0_gnn_b_gcn", "L0_gnn_W_fc", "L0_gnn_b_fc",
        "L0_ffn_Wr", "L0_ffn_W1", "L0_ffn_W2"]


def kernel(**inputs):
    import concourse.bacc as bacc
    from concourse.bass_utils import run_bass_kernel_spmd

    nc = bacc.Bacc("TRN2", target_bir_lowering=False, num_devices=1)
    arrays, args = {}, []
    for name in _INS:
        a = np.ascontiguousarray(inputs[name])
        arrays[f"in_{name}"] = a
        args.append(nc.dram_tensor(f"in_{name}", a.shape, mybir.dt.from_np(a.dtype), kind="ExternalInput").ap())
    arrays["in_constants"] = constants()
    args.append(nc.dram_tensor("in_constants", (P, NCONST), F32, kind="ExternalInput").ap())
    out = nc.dram_tensor("out", (NODES, DIM), F32, kind="ExternalOutput").ap()
    gnn_moe_kernel(nc, *args, out)
    r = run_bass_kernel_spmd(nc, [arrays], core_ids=[0])
    return r.results[0]["out"]
```

```python
from contextlib import ExitStack

import numpy as np

import concourse.bass as bass
from concourse import mybir

ALU = mybir.AluOpType
ACT = mybir.ActivationFunctionType
AX = mybir.AxisListType
F32 = mybir.dt.float32
F16 = mybir.dt.float16
BF16 = mybir.dt.bfloat16
I32 = mybir.dt.int32

P = 128
NODES, DIM, HID = 1250, 512, 128
EDGES = 41250
EXPERTS, FFN = 8, 256
EPS = 1e-5

KD = DIM // P
KF = FFN // P
TILES = -(-NODES // P)
LAST_ROWS = NODES - (TILES - 1) * P
PAD_NODES = TILES * P

GROUP = 16
GROUPS = 7
CHUNKS = 3
CT = GROUP * GROUPS
SPAN = P // GROUP
KEYS = TILES * SPAN
assert CT * CHUNKS * P >= EDGES and CT <= P
FULL_TILES = EDGES // P
REST = EDGES - FULL_TILES * P
LAST_FULL = FULL_TILES - 2 * CT
STEP = GROUP * P * NODES // EDGES
SLACK = 28
ALL_GROUPS = CHUNKS * GROUPS
HCOLS = (ALL_GROUPS - 1) * STEP + P
X_PARTS = [(0, 3), (3, 6), (6, TILES)]

SUMS = [(0, 5), (5, 4), (9, 4), (13, 4), (17, 4)]
assert all((n - 1) * STEP + P <= 512 for _, n in SUMS) and sum(n for _, n in SUMS) == ALL_GROUPS
SUM_OF = [s for s, (_, n) in enumerate(SUMS) for _ in range(n)]
SUM_ENDS = [a + n for a, n in SUMS]
COMPLETE = [(e * STEP - SLACK) // P for e in SUM_ENDS[:-1]] + [TILES]


def schedule():
    ready, begun, order = [], [], []
    for g in range(ALL_GROUPS + 1):
        for i, e in enumerate(SUM_ENDS):
            if g == min(e + 1, ALL_GROUPS):
                ready += list(range(COMPLETE[i - 1] if i else 0, COMPLETE[i]))
        order.append(advance(ready, begun, 1 if g < ALL_GROUPS else LAST_TOGETHER))
    while ready or begun:
        order.append(advance(ready, begun))
    return order


STEPS = (0, 1, None, 2, 3, 4)
LAST_STEPS = (0, 1, 2, 3, 4)
BEFORE_LAST = 6


def steps(t):
    return STEPS if t < BEFORE_LAST else LAST_STEPS


LAST_TOGETHER = 2


def advance(ready, begun, more=1):
    nodes = [(t, steps(t)[i]) for t, i in begun if steps(t)[i] is not None]
    for item in list(begun):
        item[1] += 1
        if item[1] == len(steps(item[0])):
            begun.remove(item)
    for _ in range(min(more, len(ready))):
        nodes.append((ready[0], 0))
        begun.append([ready.pop(0), 1])
    return nodes


SCHEDULE = schedule()
ROUTE_EARLY = 7
ROUTE_ROUND = next(g for g, nodes in enumerate(SCHEDULE) if (ROUTE_EARLY - 1, STEPS[-1]) in nodes)
assert all(k > 0 for nodes in SCHEDULE[ROUTE_ROUND:] for _, k in nodes)

W_SCALE = 4096.0
W_MAX = 8.0
WS = 256.0
QUAD = 4
BATCH = 8
RING = 3
LAST_GROUP_TILES = -(-(FULL_TILES + 1 - (ALL_GROUPS - 1) * GROUP) // BATCH) * BATCH
PAIRS = BATCH // 2



def tiles_in(g):
    return GROUP if g < ALL_GROUPS - 1 else LAST_GROUP_TILES


TOP = 2
SLOT_TILES = (TOP * NODES + EXPERTS * (P - 1)) // P
SLOTS = SLOT_TILES * P
MOST = 24
assert MOST * P >= TOP * NODES
EARLY = 21
BIG = float(1 << 20)

C_ID = 0
C_IOTA = C_ID + P
C_REP = C_IOTA + P
C_MASK = C_REP + P
C_START = C_MASK + GROUPS
C_DL = C_START + CHUNKS
C_LT = C_DL + 1
C_TRI = C_LT + EXPERTS * EXPERTS
C_VALID = C_TRI + P
C_M = C_VALID + TILES
C_TOKEN = C_M + SLOT_TILES * EXPERTS
NCONST = C_TOKEN + TILES


def constants():
    c = np.zeros((P, NCONST), np.float32)
    p = np.arange(P)
    c[:, C_ID:C_ID + P] = np.eye(P)
    c[:, C_IOTA:C_IOTA + P] = p[None, :]
    c[:CT, C_REP:C_REP + P] = (p[:CT, None] % GROUP) == (p[None, :] // SPAN)
    c[:CT, C_MASK:C_MASK + GROUPS] = (p[:CT, None] // GROUP) == np.arange(GROUPS)[None, :]
    c[:CT, C_START:C_START + CHUNKS] = (p[:CT, None] // GROUP) * STEP + np.arange(CHUNKS)[None, :] * (GROUPS * STEP) - SLACK
    c[:, C_DL] = p % SPAN
    i = np.arange(EXPERTS)
    c[:, C_LT:C_LT + 64] = (i[None, :] < i[:, None]).astype(np.float32).reshape(1, 64)
    c[:, C_TRI:C_TRI + P] = p[:, None] < p[None, :]
    c[:, C_VALID:C_VALID + TILES] = p[:, None] + P * np.arange(TILES)[None, :] < NODES
    node = p[:, None] + P * np.arange(TILES)[None, :]
    c[:, C_TOKEN:] = (node + 1) * (node < NODES)
    c[:, C_M:C_TOKEN] = np.repeat(np.arange(SLOT_TILES), EXPERTS)[None, :]
    return c


def gnn_moe_kernel(nc, x, src, dst, ew, w_gcn, b_gcn, w_fc, b_fc, w_r, w1, w2, const, out):
    ctx = ExitStack()
    with ctx:
        def sb(name, shape, dt=F32):
            return ctx.enter_context(nc.sbuf_tensor(name, shape, dt))

        def sem(name):
            return ctx.enter_context(nc.semaphore(name))

        cst = sb("cst", [P, NCONST])
        xs = sb("xs", [P, TILES, DIM])
        src_i = sb("src_i", [CT, CHUNKS, P], I32)
        dst_i = sb("dst_i", [CT, CHUNKS, P], I32)
        w_row = sb("w_row", [CT, CHUNKS, P])
        ROW_KEY, ROW_LO, ROW_W = range(3)
        rows = sb("rows", [CT, 3, CHUNKS, P])
        w_slow = sb("w_slow", [CT, CHUNKS, P])
        start_rel = sb("start_rel", [CT, CHUNKS])
        start_sel = sb("start_sel", [CT, CHUNKS, GROUPS])
        bad = sb("bad", [P, 1])
        bad_row = sb("bad_row", [1, 2])
        flag = sb("flag", [1, 1], I32)
        B_KEY, B_LO = 0, 1
        edge_b = sb("edge_b", [P, 2, CHUNKS * CT], F16)
        edge_w = sb("edge_w", [P, CHUNKS * CT // 2, 2, 2], F16)
        dval = sb("dval", [P, CHUNKS * GROUPS])
        iota_b = sb("iota_b", [P, P, 2], F16)
        one_src = sb("one_src", [P, RING, PAIRS, P, 2], F16)
        one_key = sb("one_key", [P, PAIRS, KEYS, 2], F16)
        key_w = sb("key_w", [P, RING, PAIRS, KEYS, 2, 2], F16)
        adj = sb("adj", [P, 2, TILES, GROUP * SPAN])
        part_h = sb("part_h", [P, HID])
        one_dst = sb("one_dst", [P, 2, P])
        hT = sb("hT", [P, HCOLS])
        wg = sb("wg", [P, KD, HID])
        wfc = sb("wfc", [P, KD, HID])
        wfcT = sb("wfcT", [P, DIM])
        bg = sb("bg", [P, 1])
        bfc = sb("bfc", [P, DIM])
        wr = sb("wr", [P, KD, EXPERTS])
        xg = sb("xg", [P, TILES, HID])
        stats = sb("stats", [P, TILES, 6])
        mv = sb("mv", [P, TILES, 2])
        std = sb("std", [P, TILES])
        rstd = sb("rstd", [P, TILES])
        nmr = sb("nmr", [P, TILES])
        xn = sb("xn", [P, TILES, DIM])
        xT = sb("xT", [P, 2, KD, P])
        stage = sb("stage", [P, 2, KD * FFN])
        w1_h = sb("w1_h", [P, EXPERTS, 2, KD, FFN], F16)
        w2_h = sb("w2_h", [P, EXPERTS, 2, KF, DIM], F16)
        lg = sb("lg", [P, TILES, EXPERTS])
        mx = sb("mx", [P, TILES])
        pr = sb("pr", [P, TILES, EXPERTS])
        sm = sb("sm", [P, TILES])
        cmp_gt = sb("cmp_gt", [P, TILES, EXPERTS, EXPERTS])
        cmp_eq = sb("cmp_eq", [P, TILES, EXPERTS, EXPERTS])
        rank = sb("rank", [P, TILES, EXPERTS])
        chosen = sb("chosen", [P, TILES, EXPERTS])
        chosen_b = sb("chosen_b", [P, TILES + 1, EXPERTS], BF16)
        tri_b = sb("tri_b", [P, P], BF16)
        ones_b = sb("ones_b", [P, P], BF16)
        n_i = sb("n_i", [P, EXPERTS], I32)
        tiles_i = sb("tiles_i", [P, EXPERTS], I32)
        tiles_f = sb("tiles_f", [P, EXPERTS])
        before = sb("before", [P, EXPERTS, EXPERTS])
        first = sb("first", [P, EXPERTS])
        first_slot = sb("first_slot", [P, EXPERTS])
        after = sb("after", [P, EXPERTS])
        slot = sb("slot", [P, TILES, EXPERTS])
        cand = sb("cand", [P, TOP, TILES, EXPERTS])
        slot_f = sb("slot_f", [P, TOP, TILES])
        slot_i = sb("slot_i", [P, TOP, TILES], I32)
        gate = sb("gate", [P, TOP, TILES])
        done_m = sb("done_m", [1, SLOT_TILES, EXPERTS])
        expert_f = sb("expert_f", [1, SLOT_TILES])
        expert_i = sb("expert_i", [1, SLOT_TILES], I32)
        used_i = sb("used_i", [1, 2], I32)
        place = sb("place", [P, 2, TOP, TILES], I32)
        place_b = sb("place_b", [P, 2, TOP, TILES], F16)
        one_row = sb("one_row", [P, TOP, TILES // 2, P, 2], F16)
        one_tile = sb("one_tile", [P, TOP, TILES, SLOT_TILES], F16)
        node_at = sb("node_at", [P, TOP, TILES, SLOT_TILES], F16)
        tile_b = sb("tile_b", [P, SLOT_TILES], F16)
        node_i = sb("node_i", [P, SLOT_TILES], I32)
        SB = 3
        xt_in = sb("xt_in", [P, SB, DIM])
        xT_h = sb("xT_h", [P, SB, 2, KD, P], F16)
        adj_flat = adj[:, :, :, :].rearrange("p a b s -> p (a b s)")
        hid = adj_flat[:, 0:SB * FFN].rearrange("p (s k n) -> p s k n", s=SB, k=KF)
        hid_h = adj_flat[:, SB * FFN:2 * SB * FFN].bitcast(F16).rearrange("p (s h k n) -> p s h k n", s=SB, h=2, k=KF)
        spare = xn[:, :, :].rearrange("p t d -> p (t d)")

        w1_flat = w1_h[:, :, :, :, :].rearrange("p e s k f -> p (e s k f)").bitcast(F32)

        def edge_scratch(i, dt=F32):
            v = w1_flat[0:CT, i * CHUNKS * P:(i + 1) * CHUNKS * P]
            return (v if dt == F32 else v.bitcast(dt)).rearrange("p (c e) -> p c e", c=CHUNKS)

        lo_i, hi_i = edge_scratch(0, I32), edge_scratch(1, I32)
        dl, rel, clip, ok_span, ok_win = (edge_scratch(i) for i in range(2, 7))
        y_first = xn
        y_second = [hT[:, 0:DIM], hT[:, DIM:2 * DIM], wfcT[:, :], bfc[:, :], wg[:, :, :].rearrange("p k h -> p (k h)"),
                    wfc[:, :, :].rearrange("p k h -> p (k h)")]
        y_second += [xT[:, i, :, :].rearrange("p k n -> p (k n)") for i in range(2)]
        y_second += [xt_in[:, i, :] for i in range(2)]
        assert len(y_second) == TILES
        y_sb = stage[:, :, :].rearrange("p b (a d) -> p (b a) d", d=DIM)

        ident = cst[:, C_ID:C_ID + P]
        iota = cst[:, C_IOTA:C_IOTA + P]

        bank = [ctx.enter_context(nc.psum_tensor(f"bank{i}", [P, 512], F32)) for i in range(8)]
        ADJ = [bank[0], bank[1], bank[6]]
        AGG = bank[2]
        FC, TURN, LOGIT, POS, HT = bank[3], bank[4], bank[5], bank[6], bank[7]
        FC_OF = [FC] * (TILES - 1) + [bank[0]]
        TURN_OF = [TURN] * (TILES - 1) + [bank[1]]
        LOGIT_OF = [LOGIT] * (TILES - 2) + [AGG, bank[6]]
        XT, HPRE, Y = bank[0:2], bank[2:4], bank[4:6]

        s_const, s_edges, s_w = sem("const_in"), sem("edges_in"), sem("w_in")
        s_x = [sem(f"x_in{i}") for i in range(3)]
        s_out = sem("out_done")
        s_pad = sem("pads_cleared")
        s_clear = sem("aggregate_cleared")
        s_stage = [sem("stage_in0"), sem("stage_in1")]
        s_split = sem("expert_weights_split")
        s_scaled = sem("expert_weights_scaled")
        s_whi = sem("expert_weights_high")
        dv = sem("vector_step")
        s_rows = sem("edge_rows_ready")
        s_edgeT = sem("edge_rows_transposed")
        s_edgesc = sem("edge_scalars_ready")
        s_flag = sem("flag_ready")
        s_dval = sem("window_rows_ready")
        s_mv = sem("norm_stats_ready")
        s_std = sem("norm_std_ready")
        s_rstd = sem("norm_scale_ready")
        s_xn = sem("normalised_ready")
        s_xnT = sem("normalised_transposed")
        s_xT = sem("transposed_copied")
        s_xT2 = sem("second_transposed_copied")
        s_xn2 = sem("second_normalised_ready")
        s_xg_ps = sem("xg_product")
        s_xg = sem("xg_ready")
        s_wfcT_ps = sem("wfc_transposed")
        s_wfcT = sem("wfc_ready")
        s_xb = sem("x_plus_bias")
        s_okey = sem("key_one_hots_ready")
        s_one = sem("one_hots_ready")
        s_adj_ps = sem("adjacency_product")
        s_adj = sem("adjacency_copied")
        s_agg_ps = sem("aggregate_product")
        s_agg = sem("aggregate_copied")
        s_odst = sem("window_one_hot_ready")
        s_comb = sem("window_product")
        s_hT = sem("aggregate_added")
        s_fc = sem("fc_product")
        s_lg_ps = sem("logits_product")
        s_lg = sem("logits_copied")
        s_sub = sem("logits_less_max")
        s_exp = sem("exp_ready")
        s_chosen = sem("chosen_ready")
        s_pos = sem("positions_product")
        s_expert = sem("slot_tile_experts_ready")
        s_filler = sem("unused_slots_written")
        s_rowout = sem("normalised_rows_stored")
        s_ones = sem("slot_row_one_hots_ready")
        s_tile_ones = sem("slot_tile_one_hots_ready")
        s_node_at = sem("nodes_at_slot_tiles_ready")
        s_node_ps = sem("slot_nodes_product")
        s_node = sem("slot_nodes_ready")
        s_xin = [sem(f"slot_rows_in{i}") for i in range(3)]
        s_turn = sem("slot_rows_transposed")
        s_xh = sem("slot_high")
        s_xl = sem("slot_low")
        s_h = sem("hidden_product")
        s_gelu = sem("gelu_ready")
        s_hh = sem("hidden_high")
        s_hl = sem("hidden_low")
        s_y = sem("expert_product")
        s_ysb = sem("expert_output_copied")
        s_yout = [sem(f"expert_output_stored{i}") for i in range(3)]
        s_first = [sem("first_outputs_in0"), sem("first_outputs_in1")]
        s_second = [sem(f"second_output_in{i}") for i in range(TILES)]
        s_acc = sem("first_expert_added")
        s_res = sem("result_ready")
        s_prep = sem("aggregate_starts_from_bias")
        s_slowT = sem("slow_transposed")
        s_slow_sc = sem("slow_scalars")
        s_slow_v = sem("slow_operand_ready")
        s_slow_p = sem("slow_product_ready")
        s_slow_add = sem("slow_added")
        s_slow_iota = sem("slow_iota")

        cut = [0]

        def carve(rows_, n):
            cut[0] += n
            return spare[0:rows_, cut[0] - n:cut[0]]

        slow_turn = carve(P, PAD_NODES)
        slow_one = carve(P, PAD_NODES)
        slow_f = carve(CT, 2 * CHUNKS * P).rearrange("p (a c e) -> p a c e", a=2, c=CHUNKS)
        slow_sc = carve(P, 3 * CHUNKS * CT).rearrange("p (a t) -> p a t", a=3)
        slow_gw = carve(P, HID)
        slow_iota = adj[:, 0, :, :].rearrange("p b n -> p (b n)")
        x_rows = nc.dram_tensor("x_rows", [PAD_NODES, DIM], F32, kind="Internal").ap()
        y_slots = nc.dram_tensor("y_slots", [SLOTS, DIM], F32, kind="Internal").ap()
        block = ctx.enter_context(nc.Block())

        def edge_view(a, t0, n):
            return a[t0 * P:(t0 + n) * P].rearrange("(t e) -> t e", e=P)

        HALF = TILES // 2
        EDGE_DMAS = 3 * (CHUNKS + 1)
        W_DMAS = 5

        @block.sync
        def _(sp):
            sp.wait_ge(s_pad, 1)
            for a, t in ((src, src_i), (dst, dst_i), (ew, w_row)):
                for c in range(CHUNKS):
                    n = CT if c < CHUNKS - 1 else LAST_FULL
                    sp.dma_start(t[0:n, c, :], edge_view(a, c * CT, n)).then_inc(s_edges, 16)
                sp.dma_start(t[LAST_FULL:LAST_FULL + 1, CHUNKS - 1, 0:REST],
                             a[FULL_TILES * P:EDGES].rearrange("(t e) -> t e", t=1)).then_inc(s_edges, 16)
            sp.wait_ge(s_pad, 2)
            a, b = X_PARTS[2][0], TILES - 1
            sp.dma_start(xs[:, a:b, :], x[a * P:b * P, :].rearrange("(t p) d -> p t d", p=P)).then_inc(s_x[2], 16)
            sp.dma_start(xs[0:LAST_ROWS, TILES - 1, :], x[(TILES - 1) * P:NODES, :]).then_inc(s_x[2], 16)
            sp.dma_start(wfc[:, :, :], w_fc.rearrange("(k p) h -> p k h", p=P)).then_inc(s_w, 16)
            sp.dma_start(bfc[:, :], b_fc.rearrange("(a n) -> a n", a=1).broadcast_to([P, DIM])).then_inc(s_w, 16)
            sp.dma_start(wr[:, :, :], w_r.rearrange("(k p) e -> p k e", p=P)).then_inc(s_w, 16)
            for n in range(2 * EXPERTS):
                e = n // 2
                if n >= 2:
                    sp.wait_ge(s_split, n - 1)
                w = w1[e].rearrange("(k p) f -> p k f", p=P) if n % 2 == 0 else w2[e].rearrange("(k p) d -> p k d", p=P)
                sp.dma_start(stage[:, n % 2, :].rearrange("p (k f) -> p k f", k=KD if n % 2 == 0 else KF), w)\
                  .then_inc(s_stage[n % 2], 16)

            for t in range(TILES):
                sp.wait_ge(s_xn2, t + 1)
                sp.dma_start(x_rows[t * P:(t + 1) * P, :], xn[:, t, :]).then_inc(s_rowout, 16)

            def store_slots(a, b):
                for m in range(a, b):
                    sp.wait_ge(s_ysb, m + 1)
                    sp.dma_start(y_slots[m * P:(m + 1) * P, :], y_sb[:, m % SB, :]).then_inc(s_yout[m % SB], 16)

            for m in range(MOST, SLOT_TILES):
                sp.dma_start(y_slots[m * P:(m + 1) * P, :], cst[:, 0:DIM]).then_inc(s_filler, 16)
            store_slots(0, MOST)
            sp.wait_ge(s_expert, 1)
            used = sp.value_load(used_i[0:1, 0:1], min_val=0, max_val=SLOT_TILES)
            with sp.If(used > MOST):
                sp.wait_ge(s_filler, 16 * (SLOT_TILES - MOST))
                store_slots(MOST, SLOT_TILES)
            sp.end_ifs()
            for t in range(TILES):
                sp.wait_ge(s_res, t + 1)
                r = P if t < TILES - 1 else LAST_ROWS
                sp.dma_start(out[t * P:t * P + r, :], xs[0:r, t, :]).then_inc(s_out, 16)
            sp.wait_ge(s_out, 16 * TILES)

        @block.gpsimd
        def _(pool):
            for t in (src_i, dst_i):
                pool.memset(t[96:CT, CHUNKS - 1, :], 0)
            pool.memset(w_row[96:CT, CHUNKS - 1, :], 0.0).then_inc(s_pad, 1)
            pool.memset(xs[96:P, TILES - 1, :], 0.0).then_inc(s_pad, 1)
            pool.wait_ge(s_pad, 2)
            pool.memset(hT[:, :], 0.0).then_inc(s_clear, 1)
            pool.wait_ge(s_w, 16 * W_DMAS)
            for t in range(TILES):
                pool.wait_ge(s_xn, t + 1)
                pool.tensor_tensor(xs[:, t, :], xs[:, t, :], bfc[:, :], ALU.add).then_inc(s_xb, 1)
            for n in range(2 * EXPERTS):
                pool.wait_ge(s_whi, n + 1)
                dest = (w1_h if n % 2 == 0 else w2_h)[:, n // 2, :, :, :].rearrange("p s k f -> p s (k f)")
                pool.tensor_tensor(dest[:, 1, :], stage[:, n % 2, :], dest[:, 0, :], ALU.subtract).then_inc(s_split, 1)
            for a in range(TOP):
                pool.wait_ge(s_tile_ones, a + 1)
                pool.tensor_tensor(node_at[:, a, :, :], one_tile[:, a, :, :],
                                   cst[:, C_TOKEN:C_TOKEN + TILES].rearrange("p (t o) -> p t o", o=1)
                                   .broadcast_to([P, TILES, SLOT_TILES]), ALU.mult).then_inc(s_node_at, 1)
            pool.wait_ge(s_rowout, 16 * TILES)
            pool.wait_ge(s_node, 1)

            def fill_slots(m):
                if m >= SB:
                    pool.wait_ge(s_turn, m - SB + 1)
                pool.indirect_dma_start(out=xt_in[:, m % SB, :], out_offset=None, in_=x_rows[:, :],
                                        in_offset=bass.IndirectOffsetOnAxis(ap=node_i[:, m:m + 1], axis=0))\
                    .then_inc(s_xin[m % SB], 16)

            def wait_stored(n):
                for i in range(SB):
                    pool.wait_ge(s_yout[i], 16 * len(range(i, n, SB)))

            def fetch_first(n):
                for t in range(TILES):
                    r = P if t < TILES - 1 else LAST_ROWS
                    pool.indirect_dma_start(out=y_first[0:r, t, :], out_offset=None, in_=y_slots[0:n * P, :],
                                            in_offset=bass.IndirectOffsetOnAxis(ap=slot_i[0:r, 0, t:t + 1], axis=0))\
                        .then_inc(s_first[t // HALF], 16)

            for m in range(MOST):
                fill_slots(m)
            wait_stored(EARLY)
            pool.wait_ge(s_expert, 1)
            last_expert = pool.value_load(used_i[0:1, 1:2], min_val=0, max_val=SLOT_TILES)
            with pool.If(last_expert <= EARLY):
                fetch_first(EARLY)
            pool.end_ifs()
            wait_stored(MOST)
            used = pool.value_load(used_i[0:1, 0:1], min_val=0, max_val=SLOT_TILES)
            with pool.If(used > MOST):
                for m in range(MOST, SLOT_TILES):
                    fill_slots(m)
                wait_stored(SLOT_TILES)
            pool.end_ifs()
            pool.wait_ge(s_filler, 16 * (SLOT_TILES - MOST))
            last_expert = pool.value_load(used_i[0:1, 1:2], min_val=0, max_val=SLOT_TILES)
            with pool.If(last_expert > EARLY):
                fetch_first(SLOT_TILES)
            pool.end_ifs()
            for t in range(TILES):
                r = P if t < TILES - 1 else LAST_ROWS
                pool.indirect_dma_start(out=y_second[t][0:r, :], out_offset=None, in_=y_slots[:, :],
                                        in_offset=bass.IndirectOffsetOnAxis(ap=slot_i[0:r, 1, t:t + 1], axis=0))\
                    .then_inc(s_second[t], 16)

        @block.scalar
        def _(act):
            act.dma_start(cst[:, :], const[:, :]).then_inc(s_const, 16)
            for i in range(2):
                a, b = X_PARTS[i]
                act.dma_start(xs[:, a:b, :], x[a * P:b * P, :].rearrange("(t p) d -> p t d", p=P)).then_inc(s_x[i], 16)
            act.dma_start(bg[:, :], b_gcn.rearrange("(p a) -> p a", a=1)).then_inc(s_w, 16)
            act.dma_start(wg[:, :, :], w_gcn.rearrange("(k p) h -> p k h", p=P)).then_inc(s_w, 16)

            def scale(n):
                act.wait_ge(s_stage[n % 2], 16 * (n // 2 + 1))
                act.activation(stage[:, n % 2, :], stage[:, n % 2, :], ACT.Copy, scale=WS).then_inc(s_scaled, 1)

            def split_high(n):
                act.wait_ge(s_scaled, n + 1)
                dest = (w1_h if n % 2 == 0 else w2_h)[:, n // 2, :, :, :].rearrange("p s k f -> p s (k f)")
                act.activation(dest[:, 0, :], stage[:, n % 2, :], ACT.Copy).then_inc(s_whi, 1)

            def copy_xg(t):
                act.wait_ge(s_xg_ps, t + 1)
                act.activation(xg[:, t, :], bank[2 + t % 2][:, 0:HID], ACT.Copy).then_inc(s_xg, 1)

            def copy_xT(t):
                act.wait_ge(s_xnT, t + 1)
                if t >= 2:
                    act.wait_ge(s_xg_ps, t - 1)
                act.activation(xT[:, t % 2, :, :], bank[t % 2][:, :].rearrange("p (k n) -> p k n", k=KD), ACT.Copy)\
                   .then_inc(s_xT, 1)

            for i, (a, b) in enumerate(X_PARTS):
                act.wait_ge(s_mv, i + 1)
                act.activation(std[:, a:b], mv[:, a:b, 1], ACT.Sqrt).then_inc(s_std, 1)
                act.wait_ge(s_rstd, i + 1)
                for t in range(a, b):
                    act.activation(xn[:, t, :], xs[:, t, :], ACT.Identity, bias=nmr[:, t:t + 1],
                                   scale=rstd[:, t:t + 1]).then_inc(s_xn, 1)
                    if t >= 1:
                        copy_xT(t - 1)
                    if t >= 3:
                        copy_xg(t - 3)
            copy_xT(TILES - 1)
            for t in range(TILES - 3, TILES):
                copy_xg(t)
            act.wait_ge(s_wfcT_ps, 1)
            act.activation(wfcT[:, :], bank[6][:, :], ACT.Copy).then_inc(s_wfcT, 1)

            def edge_group(g):
                for i in range(tiles_in(g) // QUAD):
                    if i == BATCH // QUAD and g:
                        beside_edges(g)
                    q = g * (GROUP // QUAD) + i
                    act.wait_ge(s_adj_ps, q + 1)
                    o = adj[:, g % 2, :, QUAD * i * SPAN:QUAD * (i + 1) * SPAN].rearrange("p b (t s) -> p t b s", t=QUAD)
                    act.activation(o, ADJ[q % len(ADJ)][:, 0:QUAD * KEYS].rearrange("p (t b s) -> p t b s", t=QUAD, s=SPAN),
                                   ACT.Copy, scale=1.0 / W_SCALE).then_inc(s_adj, 1)
                if tiles_in(g) == BATCH:
                    beside_edges(g)

            def beside_edges(g):
                copy_agg(g - 1)
                node_steps(g - 1, (2,))
                if g < 2 * EXPERTS + 1:
                    scale(g - 1)

            def copy_agg(g):
                act.wait_ge(s_agg_ps, g + 1)
                m = tiles_in(g) * SPAN
                act.activation(part_h[0:m, :], AGG[0:m, 0:HID], ACT.Copy).then_inc(s_agg, 1)

            def node_steps(g, kinds):
                for kind in kinds:
                    for t, k in SCHEDULE[g]:
                        if k == kind:
                            node_step(t, k)

            def node_step(t, k):
                if k == 0:
                    act.wait_ge(s_mv, 3 + t + 1)
                    act.activation(std[:, t:t + 1], mv[:, t, 1:2], ACT.Sqrt).then_inc(s_std, 1)
                if k == 1:
                    act.wait_ge(s_rstd, 3 + t + 1)
                    act.activation(xn[:, t, :], xs[:, t, :], ACT.Identity, bias=nmr[:, t:t + 1],
                                   scale=rstd[:, t:t + 1]).then_inc(s_xn2, 1)
                if k == 2:
                    act.wait_ge(s_xnT, TILES + t + 1)
                    if t >= 2:
                        act.wait_ge(s_lg_ps, t - 1)
                    act.activation(xT[:, t % 2, :, :], TURN_OF[t][:, :].rearrange("p (k n) -> p k n", k=KD), ACT.Copy)\
                       .then_inc(s_xT2, 1)

            def exp_logits(i, a, b):
                act.wait_ge(s_sub, i + 1)
                act.activation(pr[:, a:b, :], lg[:, a:b, :], ACT.Exp).then_inc(s_exp, 1)

            for g in range(ALL_GROUPS):
                edge_group(g)
                if g:
                    node_steps(g - 1, (1, 0))
                if 1 <= g < 2 * EXPERTS + 1:
                    split_high(g - 1)
            copy_agg(ALL_GROUPS - 1)
            for g in range(ALL_GROUPS - 1, len(SCHEDULE)):
                if g == ROUTE_ROUND:
                    exp_logits(0, 0, ROUTE_EARLY)
                node_steps(g, (1, 2, 0))
            exp_logits(1, ROUTE_EARLY, TILES)

            def turned_high(m):
                act.wait_ge(s_turn, m + 1)
                if m >= SB:
                    act.wait_ge(s_h, m - SB + 1)
                act.activation(xT_h[:, m % SB, 0, :, :], XT[m % 2][:, :].rearrange("p (k n) -> p k n", k=KD),
                               ACT.Copy).then_inc(s_xh, 1)

            def gelu(m):
                act.wait_ge(s_h, m + 1)
                if m >= SB:
                    act.wait_ge(s_hl, m - SB + 1)
                    act.wait_ge(s_hh, m - SB + 1)
                act.activation(hid[:, m % SB, :, :], HPRE[m % 2][:, 0:KF * P].rearrange("p (k n) -> p k n", k=KF),
                               ACT.Gelu, scale=1.0 / WS).then_inc(s_gelu, 1)

            def copy_y(m):
                act.wait_ge(s_y, m + 1)
                if m >= SB:
                    act.wait_ge(s_yout[m % SB], 16 * (m // SB))
                act.activation(y_sb[:, m % SB, :], Y[m % 2][:, :], ACT.Copy, scale=1.0 / WS).then_inc(s_ysb, 1)

            def slot_tiles(a, b):
                for i in range(a, b + 2):
                    if i < b:
                        turned_high(i)
                    if a + 1 <= i <= b:
                        gelu(i - 1)
                    if i >= a + 2:
                        copy_y(i - 2)

            slot_tiles(0, MOST)
            act.wait_ge(s_expert, 1)
            used = act.value_load(used_i[0:1, 0:1], min_val=0, max_val=SLOT_TILES)
            with act.If(used > MOST):
                slot_tiles(MOST, SLOT_TILES)
            act.end_ifs()

        @block.vector
        def _(dve):
            steps = [0]

            def step(ins):
                steps[0] += 1
                ins.then_inc(dv, 1)
                dve.wait_ge(dv, steps[0])

            def norm_stats(a, b):
                for t in range(a, b):
                    ins = dve.bn_stats(stats[:, t, :], xs[:, t, :])
                step(ins)
                for t in range(a, b):
                    ins = dve.bn_aggr(mv[:, t, :], stats[:, t, :])
                step(ins)
                dve.tensor_scalar(mv[:, a:b, 1], mv[:, a:b, 1], EPS, None, ALU.add).then_inc(s_mv, 1)

            def norm_scale(a, b, count):
                dve.wait_ge(s_std, count + 1)
                step(dve.reciprocal(rstd[:, a:b], std[:, a:b]))
                dve.scalar_tensor_tensor(out=nmr[:, a:b], in0=mv[:, a:b, 0], scalar=-1.0,
                                         in1=rstd[:, a:b], op0=ALU.mult, op1=ALU.mult).then_inc(s_rstd, 1)

            def norm_x(i):
                dve.wait_ge(s_x[i], 16 if i < 2 else 32)
                norm_stats(*X_PARTS[i])
                norm_scale(*X_PARTS[i], i)

            norm_x(0)
            dve.wait_ge(s_edges, 16 * EDGE_DMAS)
            dve.wait_ge(s_const, 16)
            dve.wait_ge(s_pad, 1)
            dve.tensor_scalar(lo_i[:, :, :], src_i[:, :, :], P - 1, None, ALU.bitwise_and)
            dve.tensor_scalar(hi_i[:, :, :], src_i[:, :, :], 7, None, ALU.logical_shift_right)
            dve.tensor_tensor(dl[:, :, :], dst_i[:, :, :], dst_i[:, :, 0:1].broadcast_to([CT, CHUNKS, P]), ALU.subtract)
            starts = cst[0:CT, C_START:C_START + CHUNKS]
            dve.tensor_tensor(rel[:, :, :], dst_i[:, :, :],
                              starts.rearrange("p (c o) -> p c o", o=1).broadcast_to([CT, CHUNKS, P]), ALU.subtract)
            step(dve.tensor_tensor(start_rel[:, :], dst_i[:, :, 0], starts, ALU.subtract))
            dve.tensor_copy(rows[:, ROW_LO, :, :], lo_i[:, :, :])
            dve.scalar_tensor_tensor(out=rows[:, ROW_KEY, :, :], in0=hi_i[:, :, :], scalar=float(SPAN),
                                     in1=dl[:, :, :], op0=ALU.mult, op1=ALU.add)
            step(dve.tensor_scalar(clip[:, :, :], dl[:, :, :], 0.0, float(SPAN - 1), ALU.max, ALU.min))
            step(dve.tensor_tensor(ok_span[:, :, :], clip[:, :, :], dl[:, :, :], ALU.is_equal))
            step(dve.tensor_scalar(clip[:, :, :], rel[:, :, :], 0.0, float(P - 1), ALU.max, ALU.min))
            step(dve.tensor_tensor(ok_win[:, :, :], clip[:, :, :], rel[:, :, :], ALU.is_equal))
            dve.tensor_scalar(clip[:, :, :], w_row[:, :, :], -W_MAX, W_MAX, ALU.max, ALU.min)
            step(dve.tensor_tensor(ok_span[:, :, :], ok_span[:, :, :], ok_win[:, :, :], ALU.mult))
            step(dve.tensor_tensor(rows[:, ROW_W, :, :], clip[:, :, :], ok_span[:, :, :], ALU.mult))
            dve.tensor_tensor(start_sel[:, :, :],
                              start_rel[:, :].rearrange("p (c o) -> p c o", o=1).broadcast_to([CT, CHUNKS, GROUPS]),
                              cst[0:CT, C_MASK:C_MASK + GROUPS].rearrange("p (o j) -> p o j", o=1)
                              .broadcast_to([CT, CHUNKS, GROUPS]), ALU.mult)
            dve.memset(bad[:, :], 0.0)
            step(dve.tensor_tensor(w_slow[:, :, :], w_row[:, :, :], rows[:, ROW_W, :, :], ALU.subtract))
            dve.tensor_reduce(bad[0:CT, :], w_slow[:, :, :], AX.XY, ALU.max, apply_absolute_value=True)\
               .then_inc(s_rows, 1)
            norm_x(1)
            dve.tensor_copy(iota_b[:, :, :], iota.rearrange("p (n o) -> p n o", o=1).broadcast_to([P, P, 2]))
            dve.tensor_copy(tile_b[:, :], iota[:, 0:SLOT_TILES])
            dve.tensor_copy(tri_b[:, :], cst[:, C_TRI:C_TRI + P])
            dve.memset(ones_b[:, :], 1.0)
            dve.memset(chosen_b[:, :, :], 0.0)
            dve.wait_ge(s_w, 16 * W_DMAS)
            dve.wait_ge(s_clear, 1)
            dve.tensor_scalar(hT[:, :], hT[:, :], bg[:, 0:1], None, ALU.add).then_inc(s_prep, 1)
            norm_x(2)
            dve.wait_ge(s_edgeT, CHUNKS + 1)
            step(dve.tensor_reduce(bad_row[:, 0:1], bank[7][0:1, P:2 * P], AX.X, ALU.max))
            step(dve.tensor_scalar(bad_row[:, 1:2], bad_row[:, 0:1], 0.0, None, ALU.is_gt))
            dve.tensor_copy(flag[:, :], bad_row[:, 1:2]).then_inc(s_flag, 1)
            dve.tensor_scalar(dval[:, :], bank[7][:, 0:CHUNKS * GROUPS], cst[:, C_DL:C_DL + 1], None, ALU.add)\
               .then_inc(s_dval, 1)
            for c in range(CHUNKS):
                col = slice(c * CT, (c + 1) * CT)
                w = bank[4 + c][:, 2 * CT:3 * CT].rearrange("p (q u) -> p q u", u=2)
                high, low = (edge_w[:, c * CT // 2:(c + 1) * CT // 2, k, :] for k in range(2))
                dve.tensor_copy(edge_b[:, :, col], bank[4 + c][:, 0:2 * CT].rearrange("p (a t) -> p a t", a=2))
                step(dve.tensor_scalar(high, w, W_SCALE, None, ALU.mult))
                dve.scalar_tensor_tensor(out=low, in0=w, scalar=W_SCALE, in1=high, op0=ALU.mult,
                                         op1=ALU.subtract).then_inc(s_edgesc, 1)
                dve.wait_ge(s_edgesc, c + 1)


            slow = dve.value_load(flag[0:1, 0:1], min_val=0, max_val=1)
            with dve.If(slow > 0):
                dve.wait_ge(s_xnT, TILES)
                dve.tensor_copy(slow_f[:, 0, :, :], src_i[:, :, :])
                dve.tensor_copy(slow_f[:, 1, :, :], dst_i[:, :, :]).then_inc(s_slow_sc, 1)
                dve.wait_ge(s_slowT, 1)
                for c in range(CHUNKS):
                    dve.tensor_copy(slow_sc[:, :, c * CT:(c + 1) * CT],
                                    bank[c][:, 0:3 * CT].rearrange("p (a t) -> p a t", a=3)).then_inc(s_slow_sc, 1)
                dve.wait_ge(s_slow_sc, 1 + CHUNKS)
                for b in range(TILES):
                    ins = dve.tensor_scalar(slow_iota[:, b * P:(b + 1) * P], iota, float(b * P), None, ALU.add)
                ins.then_inc(s_slow_iota, 1)
                dve.wait_ge(s_slow_iota, 1)
                with dve.Fori(0, FULL_TILES + 1) as t:
                    dve.tensor_scalar(slow_one[:, :], slow_iota, slow_sc[:, 0, bass.ds(t, 1)], None,
                                      ALU.is_equal).then_inc(s_slow_v, 1)
                    dve.wait_ge(s_slow_p, t * 3 + 1)
                    for b in range(3):
                        w = min(512, PAD_NODES - 512 * b)
                        dve.tensor_copy(slow_turn[:, 512 * b:512 * b + w], bank[3 + b][:, 0:w])
                    dve.tensor_scalar(slow_one[:, :], slow_iota, slow_sc[:, 1, bass.ds(t, 1)], None,
                                      ALU.is_equal).then_inc(s_slow_v, 1)
                    dve.wait_ge(s_slow_p, t * 3 + 2)
                    dve.tensor_scalar(slow_gw[:, :], bank[2][:, 0:HID], slow_sc[:, 2, bass.ds(t, 1)], None,
                                      ALU.mult).then_inc(s_slow_v, 1)
                    dve.wait_ge(s_slow_p, t * 3 + 3)
                    for b in range(3):
                        w = min(512, PAD_NODES - 512 * b)
                        ins = dve.tensor_tensor(hT[:, SLACK + 512 * b:SLACK + 512 * b + w], bank[3 + b][:, 0:w],
                                                hT[:, SLACK + 512 * b:SLACK + 512 * b + w], ALU.add)
                    ins.then_inc(s_slow_add, 1)
                    dve.wait_ge(s_slow_add, t + 1)
            dve.end_ifs()

            def edge_group(g):
                for i in range(tiles_in(g) // BATCH):
                    if i == 1 and g:
                        node_steps(g - 1, (4,))
                    b = g * (GROUP // BATCH) + i
                    r = b % RING
                    if b >= RING:
                        dve.wait_ge(s_adj_ps, (b - RING + 1) * (BATCH // QUAD))
                    t0 = b * BATCH

                    def edges(a):
                        return edge_b[:, a, t0:t0 + BATCH].rearrange("p (q o u) -> p q o u", o=1, u=2)

                    def labels(n):
                        return iota_b[:, 0:n, :].rearrange("p (o n) u -> p o n u", o=1).broadcast_to([P, PAIRS, n, 2])

                    if b:
                        dve.wait_ge(s_one, b)
                    dve.tensor_tensor(one_key[:, :, :, :], labels(KEYS),
                                      edges(B_KEY).broadcast_to([P, PAIRS, KEYS, 2]), ALU.is_equal).then_inc(s_okey, 1)
                    dve.tensor_tensor(one_src[:, r, :, :, :], labels(P),
                                      edges(B_LO).broadcast_to([P, PAIRS, P, 2]), ALU.is_equal)
                    dve.wait_ge(s_okey, b + 1)
                    wide = [P, PAIRS, KEYS, 2, 2]
                    dve.tensor_tensor(key_w[:, r, :, :, :, :],
                                      one_key[:, :, :, :].rearrange("p q n (o u) -> p q n o u", o=1).broadcast_to(wide),
                                      edge_w[:, t0 // 2:t0 // 2 + PAIRS, :, :]
                                      .rearrange("p q (o k) u -> p q o k u", o=1).broadcast_to(wide),
                                      ALU.mult).then_inc(s_one, 1)
                if g:
                    node_steps(g - 1, (1, 0) if tiles_in(g) > BATCH else (4, 1, 0))
                if g - 1 in SUM_ENDS:
                    add_sum(SUM_ENDS.index(g - 1))
                if g >= 2:
                    dve.wait_ge(s_comb, g - 1)
                dve.tensor_scalar(one_dst[:, g % 2, :], iota, dval[:, g:g + 1], None, ALU.is_equal).then_inc(s_odst, 1)

            def node_steps(g, kinds=(1, 0, 4)):
                for kind in kinds:
                    for t, k in SCHEDULE[g]:
                        if k == kind:
                            node_step(t, k)

            def add_sum(i):
                dve.wait_ge(s_comb, SUM_ENDS[i])
                n = (SUMS[i][1] - 1) * STEP + P
                cols = slice(SUMS[i][0] * STEP, SUMS[i][0] * STEP + n)
                dve.tensor_tensor(hT[:, cols], HT[:, 0:n], hT[:, cols], ALU.add).then_inc(s_hT, 1)
                dve.wait_ge(s_hT, i + 1)

            def node_step(t, k):
                if k == 0:
                    dve.wait_ge(s_fc, t + 1)
                    step(dve.tensor_tensor(xs[:, t, :], FC_OF[t][:, :], xs[:, t, :], ALU.add))
                    norm_stats(t, t + 1)
                if k == 1:
                    norm_scale(t, t + 1, 3 + t)
                if k == 4:
                    dve.wait_ge(s_lg_ps, t + 1)
                    dve.tensor_copy(lg[:, t, :], LOGIT_OF[t][:, 0:EXPERTS]).then_inc(s_lg, 1)

            def along(t2, n, inner):
                return t2.rearrange("p (n o) -> p n o", o=1).broadcast_to([P, n, inner])

            def choose(i, a, b):
                n = b - a
                square = [P, n, EXPERTS, EXPERTS]
                prob, gt, eq, rk = pr[:, a:b, :], cmp_gt[:, a:b, :, :], cmp_eq[:, a:b, :, :], rank[:, a:b, :]
                dve.wait_ge(s_lg, b)
                step(dve.tensor_reduce(mx[:, a:b], lg[:, a:b, :], AX.X, ALU.max))
                dve.tensor_tensor(lg[:, a:b, :], lg[:, a:b, :], along(mx[:, a:b], n, EXPERTS), ALU.subtract)\
                   .then_inc(s_sub, 1)
                dve.wait_ge(s_exp, i + 1)
                step(dve.tensor_reduce(sm[:, a:b], prob, AX.X, ALU.add))
                step(dve.reciprocal(sm[:, a:b], sm[:, a:b]))
                step(dve.tensor_tensor(prob, prob, along(sm[:, a:b], n, EXPERTS), ALU.mult))
                pj = prob.rearrange("p n (o j) -> p n o j", o=1).broadcast_to(square)
                pi = prob.rearrange("p n (i o) -> p n i o", o=1).broadcast_to(square)
                lt = cst[:, C_LT:C_LT + EXPERTS * EXPERTS].rearrange("p (o i j) -> p o i j", o=1, i=EXPERTS)
                dve.tensor_tensor(gt, pj, pi, ALU.is_gt)
                step(dve.tensor_tensor(eq, pj, pi, ALU.is_equal))
                step(dve.tensor_tensor(eq, eq, lt.broadcast_to(square), ALU.mult))
                step(dve.tensor_tensor(gt, gt, eq, ALU.add))
                step(dve.tensor_reduce(rk, gt, AX.X, ALU.add))
                step(dve.tensor_scalar(rk, rk, TOP - 0.5, None, ALU.is_lt))
                step(dve.tensor_tensor(chosen[:, a:b, :], rk, along(cst[:, C_VALID + a:C_VALID + b], n, EXPERTS), ALU.mult))
                dve.tensor_copy(chosen_b[:, a:b, :], chosen[:, a:b, :]).then_inc(s_chosen, 1)
                dve.tensor_tensor(prob, prob, chosen[:, a:b, :], ALU.mult)

            for g in range(ALL_GROUPS):
                edge_group(g)
            node_steps(ALL_GROUPS - 1)
            add_sum(len(SUMS) - 1)
            for g in range(ALL_GROUPS, len(SCHEDULE)):
                node_steps(g)
                if g == ROUTE_ROUND:
                    choose(0, 0, ROUTE_EARLY)
            choose(1, ROUTE_EARLY, TILES)

            dve.tensor_scalar(rank[:, :, :], chosen[:, :, :], -BIG, BIG, ALU.mult, ALU.add)
            dve.wait_ge(s_pos, 1)
            step(dve.tensor_scalar(n_i[:, :], POS[:, TILES * EXPERTS:(TILES + 1) * EXPERTS], float(P - 1), None, ALU.add))
            step(dve.tensor_scalar(tiles_i[:, :], n_i[:, :], 7, None, ALU.logical_shift_right))
            step(dve.tensor_copy(tiles_f[:, :], tiles_i[:, :]))
            step(dve.tensor_tensor(before[:, :, :],
                                   tiles_f[:, :].rearrange("p (o j) -> p o j", o=1).broadcast_to([P, EXPERTS, EXPERTS]),
                                   cst[:, C_LT:C_LT + EXPERTS * EXPERTS].rearrange("p (i j) -> p i j", i=EXPERTS), ALU.mult))
            step(dve.tensor_reduce(first[:, :], before[:, :, :], AX.X, ALU.add))
            dve.tensor_tensor(after[:, :], first[:, :], tiles_f[:, :], ALU.add)
            step(dve.tensor_scalar(first_slot[:, :], first[:, :], float(P), None, ALU.mult))
            step(dve.tensor_tensor(slot[:, :, :], POS[:, 0:TILES * EXPERTS].rearrange("p (t e) -> p t e", t=TILES),
                                   first_slot[:, :].rearrange("p (o e) -> p o e", o=1)
                                   .broadcast_to([P, TILES, EXPERTS]), ALU.add))
            dve.tensor_tensor(cand[:, 1, :, :], slot[:, :, :], chosen[:, :, :], ALU.mult)
            step(dve.tensor_tensor(cand[:, 0, :, :], slot[:, :, :], rank[:, :, :], ALU.add))
            dve.tensor_reduce(slot_f[:, 0, :], cand[:, 0, :, :], AX.X, ALU.min)
            step(dve.tensor_reduce(slot_f[:, 1, :], cand[:, 1, :, :], AX.X, ALU.max))
            step(dve.tensor_copy(slot_i[:, :, :], slot_f[:, :, :]))
            dve.tensor_scalar(place[:, 0, :, :], slot_i[:, :, :], P - 1, None, ALU.bitwise_and)
            step(dve.tensor_scalar(place[:, 1, :, :], slot_i[:, :, :], 7, None, ALU.logical_shift_right))
            step(dve.tensor_copy(place_b[:, :, :, :], place[:, :, :, :]))
            wide = [P, TILES, SLOT_TILES]
            for a in range(TOP):
                dve.tensor_tensor(one_tile[:, a, :, :],
                                  tile_b[:, :].rearrange("p (o m) -> p o m", o=1).broadcast_to(wide),
                                  place_b[:, 1, a, :].rearrange("p (t o) -> p t o", o=1).broadcast_to(wide),
                                  ALU.is_equal).then_inc(s_tile_ones, 1)
            for a in range(TOP):
                ins = dve.tensor_tensor(one_row[:, a, :, :, :],
                                  iota_b[:, :, :].rearrange("p (o n) u -> p o n u", o=1).broadcast_to([P, TILES // 2, P, 2]),
                                  place_b[:, 0, a, :].rearrange("p (q o u) -> p q o u", o=1, u=2)
                                  .broadcast_to([P, TILES // 2, P, 2]), ALU.is_equal)
            ins.then_inc(s_ones, 1)
            dve.wait_ge(s_node_ps, 1)
            dve.tensor_scalar(node_i[:, :], POS[:, 0:SLOT_TILES], -1.0, 0.0, ALU.add, ALU.max).then_inc(s_node, 1)
            step(dve.tensor_tensor(done_m[:, :, :], cst[0:1, C_M:C_M + SLOT_TILES * EXPERTS]
                                   .rearrange("p (m e) -> p m e", e=EXPERTS),
                                   after[0:1, :].rearrange("p (o e) -> p o e", o=1)
                                   .broadcast_to([1, SLOT_TILES, EXPERTS]), ALU.is_ge))
            step(dve.tensor_reduce(expert_f[:, :], done_m[:, :, :], AX.X, ALU.add))
            dve.tensor_copy(used_i[:, 0:1], after[0:1, EXPERTS - 1:EXPERTS])
            dve.tensor_copy(used_i[:, 1:2], first[0:1, EXPERTS - 1:EXPERTS])
            dve.tensor_scalar(expert_i[:, :], expert_f[:, :], float(EXPERTS - 1), None, ALU.min).then_inc(s_expert, 1)
            for a in range(TOP):
                step(dve.tensor_tensor(cand[:, a, :, :], cand[:, a, :, :], along(slot_f[:, a, :], TILES, EXPERTS),
                                       ALU.is_equal))
                step(dve.tensor_tensor(cand[:, a, :, :], cand[:, a, :, :], pr[:, :, :], ALU.mult))
                step(dve.tensor_reduce(gate[:, a, :], cand[:, a, :, :], AX.X, ALU.add))

            def turned_low(m):
                dve.wait_ge(s_xh, m + 1)
                if m >= SB:
                    dve.wait_ge(s_h, m - SB + 1)
                dve.tensor_tensor(xT_h[:, m % SB, 1, :, :], XT[m % 2][:, :].rearrange("p (k n) -> p k n", k=KD),
                                  xT_h[:, m % SB, 0, :, :], ALU.subtract).then_inc(s_xl, 1)

            def hidden_halves(m):
                dve.wait_ge(s_gelu, m + 1)
                if m >= SB:
                    dve.wait_ge(s_y, m - SB + 1)
                dve.tensor_copy(hid_h[:, m % SB, 0, :, :], hid[:, m % SB, :, :]).then_inc(s_hh, 1)
                dve.wait_ge(s_hh, m + 1)
                dve.tensor_tensor(hid_h[:, m % SB, 1, :, :], hid[:, m % SB, :, :], hid_h[:, m % SB, 0, :, :],
                                  ALU.subtract).then_inc(s_hl, 1)

            def slot_tiles(a, b):
                for i in range(a, b + 1):
                    if i < b:
                        turned_low(i)
                    if i >= a + 1:
                        hidden_halves(i - 1)

            slot_tiles(0, MOST)
            dve.wait_ge(s_expert, 1)
            used = dve.value_load(used_i[0:1, 0:1], min_val=0, max_val=SLOT_TILES)
            with dve.If(used > MOST):
                slot_tiles(MOST, SLOT_TILES)
            dve.end_ifs()

            for t in range(TILES):
                r = P if t < TILES - 1 else LAST_ROWS
                if t % HALF == 0:
                    dve.wait_ge(s_first[t // HALF], 16 * HALF)
                dve.scalar_tensor_tensor(out=xs[0:r, t, :], in0=y_first[0:r, t, :], scalar=gate[0:r, 0, t:t + 1],
                                         in1=xs[0:r, t, :], op0=ALU.mult, op1=ALU.add).then_inc(s_acc, 1)
            for t in range(TILES):
                r = P if t < TILES - 1 else LAST_ROWS
                dve.wait_ge(s_acc, t + 1)
                dve.wait_ge(s_second[t], 16)
                dve.scalar_tensor_tensor(out=xs[0:r, t, :], in0=y_second[t][0:r, :],
                                         scalar=gate[0:r, 1, t:t + 1], in1=xs[0:r, t, :],
                                         op0=ALU.mult, op1=ALU.add).then_inc(s_res, 1)

        @block.tensor
        def _(pe):
            pe.wait_ge(s_const, 16)

            def turn_edges():
                pe.wait_ge(s_rows, 1)
                for c in range(CHUNKS):
                    for a in range(3):
                        ins = pe.transpose(bank[4 + c][:, a * CT:(a + 1) * CT], rows[:, a, c, :],
                                           cst[0:CT, C_ID:C_ID + CT])
                    ins.then_inc(s_edgeT, 1)
                pe.transpose(bank[7][0:1, P:2 * P], bad[:, 0:1], ident)
                pe.matmul(bank[7][:, 0:CHUNKS * GROUPS], cst[0:CT, C_REP:C_REP + P],
                          start_sel[:, :, :].rearrange("p c j -> p (c j)"), start=True, stop=True).then_inc(s_edgeT, 1)


            def turn_x(t):
                pe.wait_ge(s_xn, t + 1)
                if t >= 2:
                    pe.wait_ge(s_xT, t - 1)
                for k in range(KD):
                    ins = pe.transpose(bank[t % 2][:, k * P:(k + 1) * P], xn[:, t, k * P:(k + 1) * P], ident)
                ins.then_inc(s_xnT, 1)

            def product_x(t):
                pe.wait_ge(s_xT, t + 1)
                if t >= 2:
                    pe.wait_ge(s_xg, t - 1)
                if t == 0:
                    pe.wait_ge(s_w, 16 * W_DMAS)
                for k in range(KD):
                    ins = pe.matmul(bank[2 + t % 2][:, 0:HID], xT[:, t % 2, k, :], wg[:, k, :],
                                    start=(k == 0), stop=(k == KD - 1))
                ins.then_inc(s_xg_ps, 1)

            for t in range(TILES + 1):
                if t < TILES:
                    turn_x(t)
                if t:
                    product_x(t - 1)
                if t == X_PARTS[0][1] - 1:
                    turn_edges()
            pe.wait_ge(s_dval, 1)
            pe.wait_ge(s_flag, 1)
            pe.wait_ge(s_edgesc, CHUNKS)
            for k in range(KD):
                ins = pe.transpose(bank[6][:, k * P:(k + 1) * P], wfc[:, k, :], ident)
            ins.then_inc(s_wfcT_ps, 1)

            slow = pe.value_load(flag[0:1, 0:1], min_val=0, max_val=1)
            with pe.If(slow > 0):
                pe.wait_ge(s_slow_sc, 1)
                pe.wait_ge(s_xg, TILES)
                for c in range(CHUNKS):
                    for a in range(3):
                        row = slow_f[:, a, c, :] if a < 2 else w_slow[:, c, :]
                        ins = pe.transpose(bank[c][:, a * CT:(a + 1) * CT], row, cst[0:CT, C_ID:C_ID + CT])
                ins.then_inc(s_slowT, 1)
                pe.wait_ge(s_slow_sc, 1 + CHUNKS)
                with pe.Fori(0, FULL_TILES + 1) as t:
                    pe.wait_ge(s_slow_v, t * 3 + 1)
                    for b in range(TILES):
                        ins = pe.transpose(bank[3 + b // 4][:, (b % 4) * P:(b % 4 + 1) * P],
                                           slow_one[:, b * P:(b + 1) * P], ident)
                    ins.then_inc(s_slow_p, 1)
                    pe.wait_ge(s_slow_v, t * 3 + 2)
                    for b in range(TILES):
                        ins = pe.matmul(bank[2][:, 0:HID], slow_turn[:, b * P:(b + 1) * P], xg[:, b, :],
                                        start=(b == 0), stop=(b == TILES - 1))
                    ins.then_inc(s_slow_p, 1)
                    pe.wait_ge(s_slow_v, t * 3 + 3)
                    for b in range(3):
                        w = min(512, PAD_NODES - 512 * b)
                        ins = pe.matmul(bank[3 + b][:, 0:w], slow_gw[:, :], slow_one[:, 512 * b:512 * b + w],
                                        start=True, stop=True)
                    ins.then_inc(s_slow_p, 1)
                pe.wait_ge(s_slow_add, FULL_TILES + 1)
            pe.end_ifs()
            pe.wait_ge(s_xg, TILES)
            pe.wait_ge(s_wfcT, 1)
            pe.wait_ge(s_xb, TILES)
            pe.wait_ge(s_prep, 1)

            def edge_group(g):
                for i in range(tiles_in(g)):
                    t = g * GROUP + i
                    if i == BATCH and g:
                        aggregate(g - 1)
                    if i % BATCH == 0:
                        pe.wait_ge(s_one, t // BATCH + 1)
                    if i % QUAD == 0 and t >= len(ADJ) * QUAD:
                        pe.wait_ge(s_adj, t // QUAD - len(ADJ) + 1)
                    o = ADJ[t // QUAD % len(ADJ)][:, i % QUAD * KEYS:(i % QUAD + 1) * KEYS]
                    r, q, u = t // BATCH % RING, i % BATCH // 2, i % 2
                    for k in range(2):
                        ins = pe.matmul(o, one_src[:, r, q, :, u], key_w[:, r, q, :, k, u],
                                        start=(k == 0), stop=(k == 1))
                    if i % QUAD == QUAD - 1:
                        ins.then_inc(s_adj_ps, 1)
                if tiles_in(g) == BATCH:
                    aggregate(g - 1)

            def aggregate(g):
                pe.wait_ge(s_adj, (g * GROUP + tiles_in(g)) // QUAD)
                m = tiles_in(g) * SPAN
                if g >= 1:
                    pe.wait_ge(s_agg, g)
                for b in range(TILES):
                    ins = pe.matmul(AGG[0:m, 0:HID], adj[:, g % 2, b, 0:m], xg[:, b, :],
                                    start=(b == 0), stop=(b == TILES - 1))
                ins.then_inc(s_agg_ps, 1)

            def combine(g):
                j = g - SUMS[SUM_OF[g]][0]
                pe.wait_ge(s_agg, g + 1)
                pe.wait_ge(s_odst, g + 1)
                if j == 0 and g:
                    pe.wait_ge(s_hT, SUM_OF[g])
                m = tiles_in(g) * SPAN
                pe.matmul(HT[:, j * STEP:j * STEP + P], part_h[0:m, :], one_dst[0:m, g % 2, :], start=(j == 0),
                          stop=(g + 1 in SUM_ENDS), skip_group_check=True).then_inc(s_comb, 1)

            def node_step(t, k):
                if k == 0:
                    if 0 < t < TILES - 1:
                        pe.wait_ge(s_mv, 3 + t)
                    pe.wait_ge(s_hT, next(i for i, n in enumerate(COMPLETE) if t < n) + 1)
                    pe.matmul(FC_OF[t][:, :], hT[:, SLACK + t * P:SLACK + (t + 1) * P], wfcT[:, :],
                              start=True, stop=True).then_inc(s_fc, 1)
                if k == 2:
                    pe.wait_ge(s_xn2, t + 1)
                    if 0 < t < TILES - 1:
                        pe.wait_ge(s_xT2, t)
                    for k in range(KD):
                        ins = pe.transpose(TURN_OF[t][:, k * P:(k + 1) * P], xn[:, t, k * P:(k + 1) * P], ident)
                    ins.then_inc(s_xnT, 1)
                elif k == 3:
                    pe.wait_ge(s_xT2, t + 1)
                    if 0 < t < TILES - 2:
                        pe.wait_ge(s_lg, t)
                    for k in range(KD):
                        ins = pe.matmul(LOGIT_OF[t][:, 0:EXPERTS], xT[:, t % 2, k, :], wr[:, k, :],
                                        start=(k == 0), stop=(k == KD - 1))
                    ins.then_inc(s_lg_ps, 1)

            for g, nodes in enumerate(SCHEDULE):
                if g < ALL_GROUPS:
                    edge_group(g)
                elif g == ALL_GROUPS:
                    aggregate(g - 1)
                if 1 <= g <= ALL_GROUPS:
                    combine(g - 1)
                kinds = (0, 3, 2, 1, 4) if g < ALL_GROUPS else (0, 2, 3, 1, 4)
                for t, k in sorted(nodes, key=lambda item: kinds.index(item[1])):
                    node_step(t, k)

            pe.wait_ge(s_chosen, 2)
            pe.matmul(POS[:, 0:(TILES + 1) * EXPERTS], tri_b[:, :], chosen_b[:, :, :].rearrange("p t e -> p (t e)"),
                      start=True, stop=False, skip_group_check=True)
            for t in range(TILES):
                n = TILES - t
                ins = pe.matmul(POS[:, (t + 1) * EXPERTS:(TILES + 1) * EXPERTS], ones_b[:, :],
                                chosen_b[:, t:t + 1, :].broadcast_to([P, n, EXPERTS]),
                                start=False, stop=(t == TILES - 1), skip_group_check=True)
            ins.then_inc(s_pos, 1)
            pe.wait_ge(s_ones, 1)
            pe.wait_ge(s_node_at, TOP)
            for a in range(TOP):
                for t in range(TILES):
                    ins = pe.matmul(POS[:, 0:SLOT_TILES], one_row[:, a, t // 2, :, t % 2], node_at[:, a, t, :],
                                    start=(a == 0 and t == 0), stop=(a == TOP - 1 and t == TILES - 1))
            ins.then_inc(s_node_ps, 1)
            pe.wait_ge(s_split, 2 * EXPERTS)
            pe.wait_ge(s_lg, TILES)
            pe.wait_ge(s_expert, 1)

            def turn(m):
                pe.wait_ge(s_xin[m % SB], 16 * (m // SB + 1))
                if m >= 2:
                    pe.wait_ge(s_xl, m - 1)
                for k in range(KD):
                    ins = pe.transpose(XT[m % 2][:, k * P:(k + 1) * P], xt_in[:, m % SB, k * P:(k + 1) * P], ident)
                ins.then_inc(s_turn, 1)

            def up(m):
                e = pe.value_load(expert_i[0:1, m:m + 1], min_val=0, max_val=EXPERTS - 1)
                pe.wait_ge(s_xh, m + 1)
                pe.wait_ge(s_xl, m + 1)
                if m >= 2:
                    pe.wait_ge(s_gelu, m - 1)
                terms = [(w_h, x_h, k) for w_h, x_h in ((0, 0), (0, 1), (1, 0)) for k in range(KD)]
                for f in range(KF):
                    for i, (w_h, x_h, k) in enumerate(terms):
                        w = w1_h[:, bass.ds(e, 1), w_h, k, f * P:(f + 1) * P].rearrange("p o f -> p (o f)")
                        ins = pe.matmul(HPRE[m % 2][:, f * P:(f + 1) * P], w, xT_h[:, m % SB, x_h, k, :],
                                        start=(i == 0), stop=(i == len(terms) - 1))
                ins.then_inc(s_h, 1)
                return e

            def down(m, e):
                pe.wait_ge(s_hh, m + 1)
                pe.wait_ge(s_hl, m + 1)
                if m >= 2:
                    pe.wait_ge(s_ysb, m - 1)
                terms = [(h_h, w_h, k) for k in range(KF) for h_h, w_h in ((0, 0), (0, 1), (1, 0))]
                for i, (h_h, w_h, k) in enumerate(terms):
                    w = w2_h[:, bass.ds(e, 1), w_h, k, :].rearrange("p o d -> p (o d)")
                    ins = pe.matmul(Y[m % 2][:, :], hid_h[:, m % SB, h_h, k, :], w,
                                    start=(i == 0), stop=(i == len(terms) - 1))
                ins.then_inc(s_y, 1)

            def slot_tiles(a, b):
                experts = {}
                for i in range(a, b + 2):
                    if i < b:
                        turn(i)
                    if a + 1 <= i <= b:
                        experts[i - 1] = up(i - 1)
                    if i >= a + 2:
                        down(i - 2, experts.pop(i - 2))

            slot_tiles(0, MOST)
            used = pe.value_load(used_i[0:1, 0:1], min_val=0, max_val=SLOT_TILES)
            with pe.If(used > MOST):
                slot_tiles(MOST, SLOT_TILES)
            pe.end_ifs()


_INS = ["x", "src", "dst", "edge_weight", "L0_gnn_W_gcn", "L0_gnn_b_gcn", "L0_gnn_W_fc", "L0_gnn_b_fc",
        "L0_ffn_Wr", "L0_ffn_W1", "L0_ffn_W2"]


def kernel(**inputs):
    import concourse.bacc as bacc
    from concourse.bass_utils import run_bass_kernel_spmd

    nc = bacc.Bacc("TRN2", target_bir_lowering=False, num_devices=1)
    arrays, args = {}, []
    for name in _INS:
        a = np.ascontiguousarray(inputs[name])
        arrays[f"in_{name}"] = a
        args.append(nc.dram_tensor(f"in_{name}", a.shape, mybir.dt.from_np(a.dtype), kind="ExternalInput").ap())
    arrays["in_constants"] = constants()
    args.append(nc.dram_tensor("in_constants", (P, NCONST), F32, kind="ExternalInput").ap())
    out = nc.dram_tensor("out", (NODES, DIM), F32, kind="ExternalOutput").ap()
    gnn_moe_kernel(nc, *args, out)
    r = run_bass_kernel_spmd(nc, [arrays], core_ids=[0])
    return r.results[0]["out"]
```
